# Optimizing a Trainium2 kernel written in Bass

```python
import numpy as np
import jax
import jax.numpy as jnp

def _softmax(x, axis=-1):
    return jax.nn.softmax(x, axis=axis)

def _gelu(x):
    return jax.nn.gelu(x, approximate=True)

def _silu(x):
    return jax.nn.silu(x)

def _sigmoid(x):
    return jax.nn.sigmoid(x)

def _layernorm(x, axis=-1, eps=1e-05):
    m = jnp.mean(x, axis=axis, keepdims=True)
    v = jnp.var(x, axis=axis, keepdims=True)
    return (x - m) / jnp.sqrt(v + eps)

def _scatter_add(tgt, idx, src, axis=0):
    return tgt.at[idx].add(src)

def _segment_sum(src, seg, n):
    return jax.ops.segment_sum(src, seg, n)
kernel_name = 'mk_sandwich_d1_jaxref_r4_b4fd83'

def setup_inputs(seed: int=0):
    np.random.seed(seed)
    _w = jnp.asarray

    def _L0_attn_setup():
        import jax, jax.numpy as jnp
        import numpy as np
        EPS = 1e-06
        N_HEADS = 16

        def _inner(x, y):
            return -x[..., 0] * y[..., 0] + jnp.sum(x[..., 1:] * y[..., 1:], axis=-1)

        def _project(x):
            sp = jnp.clip(x[..., 1:], -8.0, 8.0)
            x0 = jnp.sqrt(1.0 + jnp.sum(sp ** 2, axis=-1, keepdims=True) + EPS)
            return jnp.concatenate([x0, sp], axis=-1)

        def _exp_map(x, v):
            vx = _inner(v, x)[..., None]
            v_tan = v + vx * x
            v_ns = jnp.maximum(_inner(v_tan, v_tan), 0.0)
            v_n = jnp.minimum(jnp.sqrt(v_ns + EPS)[..., None], 5.0)
            res = jnp.cosh(v_n) * x + jnp.sinh(v_n) * v_tan / (v_n + EPS)
            return _project(res)

        def _log_map(x, y):
            y = _project(y)
            xy = jnp.minimum(_inner(x, y)[..., None], -(1.0 + EPS))
            d = jnp.maximum(jnp.arccosh(jnp.maximum(-xy, 1.0 + EPS)), 0.001)
            direc = y + xy * x
            dn = jnp.sqrt(jnp.maximum(_inner(direc, direc), EPS))[..., None]
            return d * direc / (dn + EPS)
        key = jax.random.key(seed)
        ks = jax.random.split(key, 5)
        B, T, d = (2, 256, 256)
        x = jax.random.normal(ks[0], (B, T, d), dtype=jnp.float32)
        s = 0.02
        Wq = jax.random.normal(ks[1], (d, d), dtype=jnp.float32) * s
        Wk = jax.random.normal(ks[2], (d, d), dtype=jnp.float32) * s
        Wv = jax.random.normal(ks[3], (d, d), dtype=jnp.float32) * s
        Wo = jax.random.normal(ks[4], (d, d), dtype=jnp.float32) * s
        return {'x': x, 'Wq': Wq, 'Wk': Wk, 'Wv': Wv, 'Wo': Wo}
    _L0_attn_in = _L0_attn_setup()

    def _L0_ffn_setup():
        import jax, jax.numpy as jnp
        import numpy as np
        DIM = 256

        def _reference_tuple_inner(x, W_r, W_k, W_v, mu_r, mu_k):
            B, T, C = x.shape
            x_prev = jnp.concatenate([jnp.zeros((B, 1, C), x.dtype), x[:, :-1, :]], axis=1)
            xr = mu_r * x + (1.0 - mu_r) * x_prev
            xk = mu_k * x + (1.0 - mu_k) * x_prev
            r = jax.nn.sigmoid(jnp.einsum('btc,dc->btd', xr, W_r))
            k = jnp.einsum('btc,dc->btd', xk, W_k)
            k_act = jnp.square(jax.nn.relu(k))
            out = r * jnp.einsum('btc,dc->btd', k_act, W_v)
            new_state = x[:, -1, :]
            return (out, new_state)
        key = jax.random.key(seed)
        ks = jax.random.split(key, 6)
        B, T, C = (8, 512, DIM)
        x = jax.random.normal(ks[0], (B, T, C), dtype=jnp.float32)
        s = 1.0 / np.sqrt(C)
        W_r = jax.random.uniform(ks[1], (C, C), jnp.float32, -s, s)
        W_k = jax.random.uniform(ks[2], (C, C), jnp.float32, -s, s)
        W_v = jax.random.uniform(ks[3], (C, C), jnp.float32, -s, s)
        mu_r = jax.random.uniform(ks[4], (C,), jnp.float32)
        mu_k = jax.random.uniform(ks[5], (C,), jnp.float32)
        return {'x': x, 'W_r': W_r, 'W_k': W_k, 'W_v': W_v, 'mu_r': mu_r, 'mu_k': mu_k}
    _L0_ffn_in = _L0_ffn_setup()
    _d = {'L0_attn_x': _L0_attn_in['x'], 'L0_attn_Wq': _L0_attn_in['Wq'], 'L0_attn_Wk': _L0_attn_in['Wk'], 'L0_attn_Wv': _L0_attn_in['Wv'], 'L0_attn_Wo': _L0_attn_in['Wo'], 'L0_ffn_W_r': _L0_ffn_in['W_r'], 'L0_ffn_W_k': _L0_ffn_in['W_k'], 'L0_ffn_W_v': _L0_ffn_in['W_v'], 'L0_ffn_mu_r': _L0_ffn_in['mu_r'], 'L0_ffn_mu_k': _L0_ffn_in['mu_k']}
    _x0 = _d['L0_attn_x']
    _d['L0_attn_x'] = jax.random.normal(jax.random.fold_in(jax.random.key(seed), 1), (2, 2048, 256), dtype=_x0.dtype)
    del _x0
    return _d

def reference(L0_attn_x, L0_attn_Wq, L0_attn_Wk, L0_attn_Wv, L0_attn_Wo, L0_ffn_W_r, L0_ffn_W_k, L0_ffn_W_v, L0_ffn_mu_r, L0_ffn_mu_k):

    def _L0_attn_ref(x, Wq, Wk, Wv, Wo):
        import jax, jax.numpy as jnp
        import numpy as np
        EPS = 1e-06
        N_HEADS = 16

        def _inner(x, y):
            return -x[..., 0] * y[..., 0] + jnp.sum(x[..., 1:] * y[..., 1:], axis=-1)

        def _project(x):
            sp = jnp.clip(x[..., 1:], -8.0, 8.0)
            x0 = jnp.sqrt(1.0 + jnp.sum(sp ** 2, axis=-1, keepdims=True) + EPS)
            return jnp.concatenate([x0, sp], axis=-1)

        def _exp_map(x, v):
            vx = _inner(v, x)[..., None]
            v_tan = v + vx * x
            v_ns = jnp.maximum(_inner(v_tan, v_tan), 0.0)
            v_n = jnp.minimum(jnp.sqrt(v_ns + EPS)[..., None], 5.0)
            res = jnp.cosh(v_n) * x + jnp.sinh(v_n) * v_tan / (v_n + EPS)
            return _project(res)

        def _log_map(x, y):
            y = _project(y)
            xy = jnp.minimum(_inner(x, y)[..., None], -(1.0 + EPS))
            d = jnp.maximum(jnp.arccosh(jnp.maximum(-xy, 1.0 + EPS)), 0.001)
            direc = y + xy * x
            dn = jnp.sqrt(jnp.maximum(_inner(direc, direc), EPS))[..., None]
            return d * direc / (dn + EPS)
        B, T, d = x.shape
        h = N_HEADS
        dh = d // h
        mu = jnp.zeros((d,), dtype=x.dtype).at[0].set(1.0)
        v = _log_map(mu, x)

        def proj_h(w):
            hh = w.reshape(B, T, h, dh)
            sp = jnp.clip(hh[..., 1:], -5.0, 5.0)
            x0 = jnp.sqrt(1.0 + jnp.sum(sp ** 2, axis=-1, keepdims=True) + EPS)
            return jnp.transpose(jnp.concatenate([x0, sp], axis=-1), (0, 2, 1, 3))
        q = proj_h(v @ Wq.T)
        k = proj_h(v @ Wk.T)
        vv = jnp.transpose((v @ Wv.T).reshape(B, T, h, dh), (0, 2, 1, 3))
        sc = (-jnp.einsum('bhqi,bhki->bhqk', q[..., :1], k[..., :1]) + jnp.einsum('bhqc,bhkc->bhqk', q[..., 1:], k[..., 1:])) / dh ** 0.5
        at = jax.nn.softmax(sc, axis=-1)
        out = jnp.einsum('bhqk,bhkc->bhqc', at, vv)
        out = jnp.transpose(out, (0, 2, 1, 3)).reshape(B, T, d)
        return _project(_exp_map(mu, out @ Wo.T))

    def _L0_ffn_ref(x, W_r, W_k, W_v, mu_r, mu_k):
        import jax, jax.numpy as jnp
        import numpy as np
        DIM = 256

        def _reference_tuple_inner(x, W_r, W_k, W_v, mu_r, mu_k):
            B, T, C = x.shape
            x_prev = jnp.concatenate([jnp.zeros((B, 1, C), x.dtype), x[:, :-1, :]], axis=1)
            xr = mu_r * x + (1.0 - mu_r) * x_prev
            xk = mu_k * x + (1.0 - mu_k) * x_prev
            r = jax.nn.sigmoid(jnp.einsum('btc,dc->btd', xr, W_r))
            k = jnp.einsum('btc,dc->btd', xk, W_k)
            k_act = jnp.square(jax.nn.relu(k))
            out = r * jnp.einsum('btc,dc->btd', k_act, W_v)
            new_state = x[:, -1, :]
            return (out, new_state)
        return _reference_tuple_inner(x, W_r, W_k, W_v, mu_r, mu_k)[0]
    x = L0_attn_x
    x = x + _layernorm(_L0_attn_ref(_layernorm(x, axis=-1), L0_attn_Wq, L0_attn_Wk, L0_attn_Wv, L0_attn_Wo), axis=-1)
    x = x + _layernorm(_L0_ffn_ref(_layernorm(x, axis=-1), L0_ffn_W_r, L0_ffn_W_k, L0_ffn_W_v, L0_ffn_mu_r, L0_ffn_mu_k), axis=-1)
    return x

_drawn_inputs = setup_inputs


def setup_inputs(seed=0):
    import zlib

    import numpy as np

    out = dict(_drawn_inputs(seed))
    spreads = {}
    factors = {'L0_attn_Wq': 8.0, 'L0_attn_Wk': 8.0, 'L0_attn_Wv': 8.0, 'L0_attn_Wo': 8.0}
    for name, (base, spread) in spreads.items():
        noise = np.random.default_rng([zlib.crc32(name.encode()), seed]).standard_normal(out[name].shape)
        drawn = base * np.exp(spread * noise) if base else spread * noise
        out[name] = jnp.asarray(drawn.astype(out[name].dtype))
    for name, factor in factors.items():
        out[name] = (out[name] * factor).astype(out[name].dtype)
    return out
```

```python
from contextlib import ExitStack

import concourse.bass as bass
from concourse import mybir

P = 128
F32 = mybir.dt.float32
BF16 = mybir.dt.bfloat16
ACT = mybir.ActivationFunctionType
ALU = mybir.AluOpType
AX_X = mybir.AxisListType.X

B, T, D, H = 2, 2048, 256, 16
DH = D // H
HEADS = B * H
BLOCKS = B * T // P
KB = T // P
CB = 4
BC = KB // CB
CHUNKS = B * BC
CT = CB * P
KT = D // P
PARTS = 3
PAIRS = ((0, 0), (0, 1), (0, 2), (1, 0), (1, 1), (2, 0))
ROWS = len(PAIRS) * DH
GROUP = 4
NG = T // GROUP
VW = 32
QC = T // CT
EPS = 1e-6
LN_EPS = 1e-5
SHIFT = 65.0
SINH_TERMS = 14
FREE = 1
LOADS = 2 * len(PAIRS)


def sandwich(nc, x, wq, wk, wv, wo, wr, wkf, wvf, mus, ident, headsum, cols, diag, out):
    with ExitStack() as ctx:
        def sb(name, shape, dt=F32):
            return ctx.enter_context(nc.sbuf_tensor(name, shape, dt))

        def sem(name):
            return ctx.enter_context(nc.semaphore(name))

        q_parts = nc.dram_tensor("q_parts", (PARTS, HEADS, DH, T), BF16, kind="Internal").ap()
        k_parts = nc.dram_tensor("k_parts", (PARTS, HEADS, DH, T), BF16, kind="Internal").ap()

        w_sb = {n: sb(f"w_{n}", [P, KT, D]) for n in ("q", "k", "v", "o", "r", "kf", "vf")}
        ident_sb = sb("ident_sb", [P, P])
        headsum_sb = sb("headsum_sb", [P, P])
        cols_sb = sb("cols_sb", [P, 4])
        diag_sb = sb("diag_sb", [KB, KB])
        mu_sb = sb("mu_sb", [P, 2, KT])
        omu_sb = sb("omu_sb", [P, 2, KT])
        one_eps = sb("one_eps", [P, 1])
        ln_eps = sb("ln_eps", [P, 1])
        eps_col = sb("eps_col", [P, 1])
        one_col = sb("one_col", [P, 1])

        x_sb = sb("x_sb", [P, BLOCKS, D])
        y_sb = sb("y_sb", [P, BLOCKS, D])
        v_sb = sb("v_sb", [P, BLOCKS, D])
        by_head = "p (g k i) -> p g k i"
        v_heads = v_sb[:, :, :].rearrange("p a b -> p (a b)").rearrange(by_head, g=HEADS, k=KB)
        o_heads = y_sb[:, :, :].rearrange("p a b -> p (a b)").rearrange(by_head, g=HEADS, k=KB)

        work = sb("work", [P, 4 * T])
        clipped, root, lifted, rest = (work[:, n * T:(n + 1) * T].rearrange("p (t n) -> p t n", t=4)
                                       for n in range(4))
        probs = work[:, :].rearrange("p (n q) -> p n q", n=4)
        xT = work[:, 0:2 * KT * (CT + 1)].rearrange("p (b k t) -> p b k t", b=2, k=KT)
        mixed = work[:, T + 16:3 * T + 16].rearrange("p (b w k t) -> p b w k t", b=2, w=2, k=KT)
        mix_prev = v_sb[:, :, :].rearrange("p a b -> p (a b)")[:, 0:4 * KT * CT].rearrange(
            "p (b w k t) -> p b w k t", b=2, w=2, k=KT)
        token = sb("token", [P, 2, CB, D])
        vT = sb("vT", [P, 2, KT, CT])
        square = sb("square", [P, 4, CT])
        parts = sb("parts", [P, 4, PARTS, CT], BF16)

        qT = sb("qT", [P, 2, T], BF16)
        kT = sb("kT", [P, 2, T], BF16)
        half_sums = parts[0:ROWS, 0, 0:2, :]
        group_sums = parts[0:ROWS, 1, 0:2, :]
        v_head = sb("v_head", [P, 2, KB, VW])
        group_max = sb("group_max", [P, 2, KB])
        shift_row = sb("shift_row", [KB, P])
        oT = vT[:, :, 0, :]
        rden = sb("rden", [P, 2, CB, QC])

        stats = sb("stats", [P, BLOCKS, 6])
        mv = sb("mv", [P, 2, 5, CB])
        sc = {n: sb(f"sc_{n}", [P, BLOCKS]) for n in
              ("sd", "rstd", "ss", "y0", "z", "zm", "t", "u", "w", "d", "d0", "inn", "f", "a", "dn", "mean", "var")}

        ps = ctx.enter_context(nc.psum_tensor("ps", [P, 8, CT], F32))

        s_const = sem("s_const")
        s_memset = sem("s_memset")
        s_omu = sem("s_omu")
        s_x = [sem("s_x0"), sem("s_x1")]
        s_bn = sem("s_bn")
        s_sums = sem("s_sums")
        s_diff = sem("s_diff")
        s_stats = sem("s_stats")
        s_sd = sem("s_sd")
        s_rstd = sem("s_rstd")
        s_norm = sem("s_norm")
        s_clip = sem("s_clip")
        s_ss = sem("s_ss")
        s_link = sem("s_link")
        s_logs = sem("s_logs")
        s_acts = sem("s_acts")
        s_token = sem("s_token")
        s_tr = sem("s_tr")
        s_trc = [sem("s_trc0"), sem("s_trc1")]
        s_vps = sem("s_vps")
        s_vcopy = sem("s_vcopy")
        s_proj = sem("s_proj")
        s_clipped = sem("s_clipped")
        s_square = sem("s_square")
        s_norm2 = sem("s_norm2")
        s_root = sem("s_root")
        s_lifted = sem("s_lifted")
        s_p0 = sem("s_p0")
        s_rest = sem("s_rest")
        s_p1 = sem("s_p1")
        s_p2 = sem("s_p2")
        s_store = [sem(f"s_store{n}") for n in range(4)]
        s_qk = [sem("s_qk0"), sem("s_qk1")]
        s_half = sem("s_half")
        s_gsum = sem("s_gsum")
        s_vhead = sem("s_vhead")
        s_gps = sem("s_gps")
        s_gmax = sem("s_gmax")
        s_shT = sem("s_shT")
        s_shrow = sem("s_shrow")
        s_shift = sem("s_shift")
        s_scores = sem("s_scores")
        s_exp = sem("s_exp")
        s_pv = sem("s_pv")
        s_oT = sem("s_oT")
        s_otr = sem("s_otr")
        s_rden = sem("s_rden")
        s_out = sem("s_out")
        e_token = sem("e_token")
        e_tr = sem("e_tr")
        e_trc = [sem("e_trc0"), sem("e_trc1")]
        e_wo = sem("e_wo")
        e_woc = sem("e_woc")
        e_ss = sem("e_ss")
        e_scaled = sem("e_scaled")
        e_y = sem("e_y")
        e_ss2 = sem("e_ss2")
        e_bn = sem("e_bn")
        e_smalls = sem("e_smalls")
        e_x1 = sem("e_x1")
        f_token = sem("f_token")
        f_tr = sem("f_tr")
        f_trc = [sem("f_trc0"), sem("f_trc1")]
        f_edge = sem("f_edge")
        f_prev = sem("f_prev")
        f_mix = sem("f_mix")
        f_r = sem("f_r")
        f_k = sem("f_k")
        f_relu = sem("f_relu")
        f_sq = sem("f_sq")
        f_kv = sem("f_kv")
        f_sig = sem("f_sig")
        f_o = sem("f_o")
        f_bn = sem("f_bn")
        f_out = sem("f_out")
        s_done = sem("s_done")

        frees = s_store + s_trc + e_trc + f_trc + [s_tr, s_lifted, s_sd, s_clipped, s_root, s_vcopy, e_tr, e_woc,
                                                   f_mix, f_sq, f_o, f_tr, f_r, f_relu, f_sig, f_kv]
        N_CONST = 5 + len(w_sb)
        x_blocks = x.rearrange("(n p) d -> p n d", p=P)
        out_blocks = out.rearrange("(n p) d -> p n d", p=P)

        def blocks(t, first, n=1):
            return t[:, bass.ds(first, n), :].rearrange("p n d -> p (n d)")

        block = ctx.enter_context(nc.Block())

        @block.sync
        def _(sp):
            for free in frees:
                sp.sem_inc(free, FREE)
            for c in range(2):
                sp.dma_start(x_sb[:, c * CB:(c + 1) * CB, :],
                             x_blocks[:, c * CB:(c + 1) * CB, :]).then_inc(s_x[c], 16)
            with sp.Fori(1, CHUNKS // 2) as i:
                for c in range(2):
                    sp.wait_ge(s_x[c], i * 16)
                    sp.dma_start(x_sb[:, bass.ds((i * 2 + c) * CB, CB), :],
                                 x_blocks[:, bass.ds((i * 2 + c) * CB, CB), :]).then_inc(s_x[c], 16)
            for t, a in ((ident_sb, ident), (headsum_sb, headsum), (cols_sb, cols), (diag_sb, diag)):
                sp.dma_start(t[:, :], a).then_inc(s_const, 16)
            sp.dma_start(mu_sb[:, :, :], mus).then_inc(s_const, 16)
            for n, a in (("q", wq), ("k", wk), ("v", wv), ("o", wo), ("r", wr), ("kf", wkf), ("vf", wvf)):
                sp.dma_start(w_sb[n][:, :, :], a.rearrange("(k p) d -> p k d", p=P)).then_inc(s_const, 16)
            with sp.Fori(0, B) as b:
                for cc in range(BC):
                    for t in range(4):
                        rows = (q_parts, k_parts)[t // 2].rearrange("s g i t -> (g i) s t")
                        n = b * (4 * BC) + (cc * 4 + t + 1)
                        sp.wait_ge(s_p0, n)
                        sp.wait_ge(s_p1, n)
                        sp.wait_ge(s_p2, n)
                        sp.dma_start(rows[bass.ds(b * D + (t % 2) * P, P), :, cc * CT:(cc + 1) * CT],
                                     parts[:, t, :, :]).then_inc(s_store[t], 16)
            for t in range(4):
                sp.wait_ge(s_store[t], FREE + 16 * CHUNKS)

            def load_head(g, buf):
                for n, (pq, pk) in enumerate(PAIRS):
                    r = slice(n * DH, (n + 1) * DH)
                    for dst, src in ((qT, q_parts[pq]), (kT, k_parts[pk])):
                        sp.dma_start(dst[r, buf, :], src[bass.ds(g, 1), :, :].rearrange("g i t -> (g i) t")
                                     ).then_inc(s_qk[buf], 16)

            load_head(0, 0)
            load_head(1, 1)
            with sp.Fori(1, HEADS // 2) as i:
                for buf in range(2):
                    sp.wait_ge(s_scores, i * (4 * KB) + (buf - 1) * 2 * KB)
                    load_head(i * 2 + buf, buf)
            with sp.Fori(0, CHUNKS) as c:
                sp.wait_ge(f_out, c + 1)
                sp.dma_start(out_blocks[:, bass.ds(c * CB, CB), :],
                             y_sb[:, bass.ds(c * CB, CB), :]).then_inc(s_done, 16)
            sp.wait_ge(s_done, 16 * CHUNKS)

        @block.gpsimd
        def _(pool):
            nc.gpsimd.memset(one_eps[:, :], 1.0 + EPS).then_inc(s_memset, 1)
            nc.gpsimd.memset(ln_eps[:, :], LN_EPS).then_inc(s_memset, 1)
            nc.gpsimd.memset(eps_col[:, :], EPS).then_inc(s_memset, 1)
            nc.gpsimd.memset(one_col[:, :], 1.0).then_inc(s_memset, 1)
            nc.gpsimd.memset(v_head[:, :, :, DH + 1:VW], 0.0).then_inc(s_memset, 1)
            nc.gpsimd.memset(v_head[:, :, :, DH:DH + 1], 1.0).then_inc(s_memset, 1)

            pool.wait_ge(s_memset, 6)
            nc.gpsimd.memset(kT[ROWS:ROWS + KB, :, :], 1.0).then_inc(s_memset, 1)
            pool.wait_ge(s_memset, 7)

            with pool.Fori(0, B) as b:
                for cc in range(BC):
                    tile0 = b * 4 * BC + cc * 4
                    for t in range(5):
                        if t < 4:
                            pool.wait_ge(s_root, FREE + tile0 + (t + 1))
                            nc.gpsimd.tensor_tensor(lifted[:, t, :], clipped[:, t, :], root[:, t, :],
                                                    ALU.subtract if t < 2 else ALU.add).then_inc(s_lifted, 1)
                        if t >= 1:
                            pool.wait_ge(s_p0, tile0 + t)
                            nc.gpsimd.tensor_tensor(rest[:, t - 1, :], lifted[:, t - 1, :], parts[:, t - 1, 0, :],
                                                    ALU.subtract).then_inc(s_rest, 1)

            pool.wait_ge(s_memset, 7)
            pool.wait_ge(s_vcopy, FREE + 2 * CHUNKS)

            def load_v(g, buf):
                v = v_heads[:, bass.ds(g, 1), :, :].rearrange("p g k i -> p (g k) i")
                nc.gpsimd.tensor_tensor(v_head[:, buf, :, 0:DH], v, one_col[:, :].unsqueeze(2).broadcast_to([P, KB, DH]),
                                        ALU.mult).then_inc(s_vhead, 1)

            load_v(0, 0)
            load_v(1, 1)
            with pool.Fori(1, HEADS // 2) as i:
                for buf in range(2):
                    pool.wait_ge(s_pv, i * (2 * KB) + (buf - 1) * KB)
                    load_v(i * 2 + buf, buf)

            with pool.Fori(0, CHUNKS) as c:
                pool.wait_ge(f_kv, FREE + c * 2)
                for dt in range(KT):
                    pool.wait_ge(f_relu, FREE + c * KT + (dt + 1))
                    nc.gpsimd.tensor_tensor(square[:, 2 + dt, :], square[:, dt, :], square[:, dt, :],
                                            ALU.mult).then_inc(f_sq, 1)

        @block.scalar
        def _(act):
            act.wait_ge(s_memset, 7)

            def row_norms(src, ready, done, c, base):
                act.wait_ge(ready, base + 1)
                for j in range(CB):
                    blk = c * CB + j
                    nc.scalar.activation(square[:, 0, 1:D], src[:, bass.ds(blk, 1), 1:D].rearrange("p n d -> p (n d)"),
                                         ACT.Square, accum_out=sc["ss"][:, bass.ds(blk, 1)]).then_inc(done, 1)
                    act.wait_ge(done, blk + 1)

            def norm_sd(b, cc):
                act.wait_ge(s_stats, b * BC + (cc + 1))
                nc.scalar.activation(sc["sd"][:, bass.ds(b * KB + cc * CB, CB)],
                                     mv[:, cc % 2, 1, :], ACT.Sqrt,
                                     bias=ln_eps[:, 0:1]).then_inc(s_sd, 1)

            with act.Fori(0, B) as b:
                norm_sd(b, 0)
                for cc in range(BC):
                    if cc + 1 < BC:
                        norm_sd(b, cc + 1)
                    row_norms(y_sb, s_clip, s_ss, b * BC + cc, b * BC + cc)

            nc.scalar.activation(sc["y0"][:, :], sc["ss"][:, :], ACT.Sqrt, bias=one_eps[:, 0:1]).then_inc(s_acts, 1)
            act.wait_ge(s_logs, 1)
            nc.scalar.activation(sc["u"][:, :], sc["t"][:, :], ACT.Sqrt).then_inc(s_acts, 1)
            act.wait_ge(s_logs, 2)
            nc.scalar.activation(sc["dn"][:, :], sc["inn"][:, :], ACT.Sqrt).then_inc(s_acts, 1)
            nc.scalar.activation(sc["d"][:, :], sc["w"][:, :], ACT.Ln).then_inc(s_acts, 1)

            act.wait_ge(s_const, 16 * N_CONST)
            with act.Fori(0, B) as b:
                for cc in range(BC):
                    par = cc % 2
                    tile0 = b * 4 * BC + cc * 4

                    def make_square(t):
                        act.wait_ge(s_clipped, FREE + tile0 + (t + 1))
                        nc.scalar.activation(square[:, t, :], clipped[:, t, :], ACT.Square).then_inc(s_square, 1)

                    def make_root(t):
                        act.wait_ge(s_norm2, tile0 + (t + 1))
                        nc.scalar.activation(root[:, t, :], ps[:, 2 + t % 2, :], ACT.Sqrt,
                                             bias=cols_sb[:, 2:3]).then_inc(s_root, 1)

                    def part0(t):
                        act.wait_ge(s_lifted, FREE + tile0 + (t + 1))
                        act.wait_ge(s_store[t], FREE + b * 16 * BC + 16 * cc)
                        nc.scalar.activation(parts[:, t, 0, :], lifted[:, t, :], ACT.Copy).then_inc(s_p0, 1)

                    def v_copy(n):
                        act.wait_ge(s_vps, b * 2 * BC + (cc * 2 + n + 1))
                        for j in range(2):
                            kb = cc * CB + n * 2 + j
                            last = nc.scalar.activation(
                                v_heads[:, bass.ds(b * H, H), kb:kb + 1, :].rearrange("p h k i -> p h (k i)"),
                                ps[:, 6 + n, j * D:(j + 1) * D].rearrange("p (h i) -> p h i", h=H), ACT.Copy)
                        last.then_inc(s_vcopy, 1)

                    act.wait_ge(s_tr, FREE + b * 2 * BC + (cc * 2 + 1))
                    nc.scalar.activation(vT[:, par, 0, :], ps[:, 4, :], ACT.Copy).then_inc(s_trc[0], 1)
                    make_square(0)
                    make_root(0)
                    make_square(1)
                    v_copy(0)
                    make_root(1)
                    make_square(2)
                    part0(0)
                    v_copy(1)
                    make_root(2)
                    make_square(3)
                    part0(1)
                    make_root(3)
                    part0(2)
                    part0(3)

            def exps(g, first):
                for kb in range(KB):
                    for half in range(2):
                        act.wait_ge(s_scores, g * (2 * KB) + (kb * 2 + half + 1))
                        if not first or kb >= 4:
                            act.wait_ge(s_pv, g * KB + (kb - 3))
                        nc.scalar.activation(
                            probs[:, kb % 4, half * 2 * CT:(half + 1) * 2 * CT].rearrange("p (a q) -> p a q", a=2),
                            ps[:, half * 2:half * 2 + 2, :], ACT.Exp, scale=DH ** -0.5).then_inc(s_exp, 1)

            exps(0, True)
            with act.Fori(0, HEADS // 2 - 1) as i:
                exps(i * 2 + 1, False)
                exps(i * 2 + 2, False)
            exps(HEADS - 1, False)

            with act.Fori(0, B) as b:
                for cc in range(BC):
                    act.wait_ge(e_tr, FREE + b * 2 * BC + (cc * 2 + 1))
                    nc.scalar.activation(vT[:, cc % 2, 0, :], ps[:, 4, :], ACT.Copy).then_inc(e_trc[0], 1)
                    row_norms(v_sb, e_woc, e_ss, b * BC + cc, FREE + b * 2 * BC + (cc * 2 + 1))
            nc.scalar.activation(sc["u"][:, :], sc["ss"][:, :], ACT.Sqrt, bias=eps_col[:, 0:1]).then_inc(s_acts, 1)
            with act.Fori(0, CHUNKS) as c:
                row_norms(v_sb, e_y, e_ss2, c, c)
            nc.scalar.activation(sc["y0"][:, :], sc["ss"][:, :], ACT.Sqrt, bias=one_eps[:, 0:1]).then_inc(s_acts, 1)
            for n in range(2):
                act.wait_ge(e_smalls, n + 1)
                nc.scalar.activation(sc["sd"][:, :], sc["var"][:, :], ACT.Sqrt, bias=ln_eps[:, 0:1]).then_inc(s_acts, 1)

            with act.Fori(0, B) as b:
                def to_xT(cc):
                    act.wait_ge(f_tr, FREE + b * 2 * BC + (cc * 2 + 1))
                    act.wait_ge(f_mix, FREE + b * BC + max(cc - 1, 0))
                    nc.scalar.activation(xT[:, cc % 2, 0, 1:CT + 1], ps[:, 4, :], ACT.Copy).then_inc(f_trc[0], 1)

                to_xT(0)
                for cc in range(BC):
                    if cc + 1 < BC:
                        to_xT(cc + 1)
                    for dt in range(KT):
                        act.wait_ge(f_k, b * KT * BC + (cc * KT + dt + 1))
                        act.wait_ge(f_sq, FREE + b * KT * BC + cc * KT)
                        nc.scalar.activation(square[:, dt, :], ps[:, 2 + dt, :], ACT.Relu).then_inc(f_relu, 1)
                    act.wait_ge(f_r, FREE + b * BC + (cc + 1))
                    act.wait_ge(f_o, FREE + b * BC + max(cc - 1, 0))
                    nc.scalar.activation(vT[:, cc % 2, :, :], ps[:, 0:2, :], ACT.Sigmoid).then_inc(f_sig, 1)
            act.wait_ge(e_smalls, 3)
            nc.scalar.activation(sc["sd"][:, :], sc["var"][:, :], ACT.Sqrt, bias=ln_eps[:, 0:1]).then_inc(s_acts, 1)

        @block.vector
        def _(dve):
            links = [0]

            def link(ins):
                links[0] += 1
                ins.then_inc(s_link, 1)
                dve.wait_ge(s_link, links[0])

            def layer_stats(src, done, c):
                for j in range(CB):
                    last = nc.vector.bn_stats(stats[:, bass.ds(c * CB + j, 1), :].rearrange("p n s -> p (n s)"),
                                              blocks(src, c * CB + j))
                last.then_inc(done, 1)

            def combine_stats():
                even, odd, m2_even, m2_odd = (stats[:, :, n:n + 1].rearrange("p n o -> p (n o)") for n in (1, 4, 2, 5))
                link(nc.vector.tensor_tensor(s["a"], even, odd, ALU.subtract))
                link(nc.vector.tensor_tensor(s["w"], m2_even, m2_odd, ALU.add))
                link(nc.vector.tensor_tensor(s["z"], even, odd, ALU.add))
                link(nc.vector.scalar_tensor_tensor(s["a"], s["a"], 0.25, s["a"], ALU.mult, ALU.mult))
                link(nc.vector.tensor_scalar(s["mean"], s["z"], 0.5, None, ALU.mult))
                nc.vector.scalar_tensor_tensor(s["var"], s["w"], 1.0 / D, s["a"], ALU.mult, ALU.add).then_inc(e_smalls, 1)

            def normalise(dst, src, mean, c):
                for j in range(CB):
                    blk = c * CB + j
                    last = nc.vector.tensor_scalar(dst(j), blocks(src, blk),
                                                   mean(j),
                                                   sc["rstd"][:, bass.ds(blk, 1)], ALU.subtract, ALU.mult)
                return last

            with dve.Fori(0, B) as b:
                def norm_stats(cc):
                    dve.wait_ge(s_x[cc % 2], b * 8 * BC + 16 * (cc // 2 + 1))
                    dve.wait_ge(s_sd, FREE + b * BC + max(cc - 1, 0))
                    for j in range(CB):
                        last = nc.vector.bn_stats(stats[:, cc % 2 * CB + j, :], blocks(x_sb, b * KB + (cc * CB + j)))
                    last.then_inc(s_bn, 1)
                    dve.wait_ge(s_bn, b * BC + (cc + 1))
                    even, odd, m2_even, m2_odd = (
                        stats[:, cc % 2 * CB:cc % 2 * CB + CB, n:n + 1].rearrange("p n o -> p (n o)") for n in (1, 4, 2, 5))
                    diff, both, m2 = (mv[:, cc % 2, n, :] for n in (2, 3, 4))
                    nc.vector.tensor_tensor(diff, even, odd, ALU.subtract)
                    nc.vector.tensor_tensor(m2, m2_even, m2_odd, ALU.add)
                    nc.vector.tensor_tensor(both, even, odd, ALU.add).then_inc(s_sums, 1)
                    dve.wait_ge(s_sums, b * BC + (cc + 1))
                    nc.vector.tensor_scalar(mv[:, cc % 2, 0, :], both, 0.5, None, ALU.mult)
                    nc.vector.scalar_tensor_tensor(diff, diff, 0.25, diff, ALU.mult, ALU.mult).then_inc(s_diff, 1)
                    dve.wait_ge(s_diff, b * BC + (cc + 1))
                    nc.vector.scalar_tensor_tensor(mv[:, cc % 2, 1, :], m2, 1.0 / D, diff, ALU.mult,
                                                   ALU.add).then_inc(s_stats, 1)

                norm_stats(0)
                for cc in range(BC):
                    c = b * BC + cc
                    if cc + 1 < BC:
                        norm_stats(cc + 1)
                    dve.wait_ge(s_sd, FREE + c + 1)
                    nc.vector.reciprocal(sc["rstd"][:, bass.ds(c * CB, CB)],
                                         sc["sd"][:, bass.ds(c * CB, CB)]).then_inc(s_rstd, 1)
                    dve.wait_ge(s_rstd, c + 1)
                    normalise(lambda j, c=c: blocks(y_sb, c * CB + j), x_sb,
                              lambda j, cc=cc: mv[:, cc % 2, 0, j:j + 1], c).then_inc(s_norm, 1)
                    dve.wait_ge(s_norm, c + 1)
                    nc.vector.tensor_scalar(blocks(y_sb, c * CB, CB), blocks(y_sb, c * CB, CB),
                                            8.0, -8.0, ALU.min, ALU.max).then_inc(s_clip, 1)

            s = {n: t[:, :] for n, t in sc.items()}
            dve.wait_ge(s_acts, 1)
            link(nc.vector.tensor_scalar(s["z"], s["y0"], 1.0 + EPS, None, ALU.max))
            link(nc.vector.tensor_scalar(s["zm"], s["z"], -1.0, None, ALU.add))
            nc.vector.scalar_tensor_tensor(s["t"], s["z"], 1.0, s["zm"], ALU.add, ALU.mult).then_inc(s_logs, 1)
            link(nc.vector.tensor_tensor(s["d0"], s["y0"], s["z"], ALU.subtract))
            link(nc.vector.tensor_tensor(s["a"], s["d0"], s["d0"], ALU.mult))
            link(nc.vector.tensor_tensor(s["inn"], s["ss"], s["a"], ALU.subtract))
            link(nc.vector.tensor_scalar(s["inn"], s["inn"], EPS, None, ALU.max))
            dve.wait_ge(s_acts, 2)
            nc.vector.tensor_tensor(s["w"], s["z"], s["u"], ALU.add).then_inc(s_logs, 1)
            link(nc.vector.tensor_copy(y_sb[:, :, 0:1].rearrange("p n o -> p (n o)"), s["d0"]))
            dve.wait_ge(s_acts, 3)
            link(nc.vector.tensor_scalar(s["dn"], s["dn"], EPS, None, ALU.add))
            link(nc.vector.reciprocal(s["dn"], s["dn"]))
            dve.wait_ge(s_acts, 4)
            link(nc.vector.scalar_tensor_tensor(s["f"], s["d"], 0.001, s["dn"], ALU.max, ALU.mult))

            dve.wait_ge(s_const, 16 * N_CONST)
            nc.vector.tensor_scalar(omu_sb[:, :, :], mu_sb[:, :, :], -1.0, 1.0, ALU.mult, ALU.add).then_inc(s_omu, 1)

            with dve.Fori(0, B) as b:
                def to_token(cc):
                    dve.wait_ge(s_tr, FREE + b * 2 * BC + max(2 * (cc - 1), 0))
                    for j in range(CB):
                        blk = b * KB + (cc * CB + j)
                        last = nc.vector.tensor_scalar(token[:, cc % 2, j, :], blocks(y_sb, blk),
                                                       sc["f"][:, bass.ds(blk, 1)], None, ALU.mult)
                    last.then_inc(s_token, 1)

                to_token(0)
                for cc in range(BC):
                    tile0 = b * 4 * BC + cc * 4

                    def clip(t):
                        dve.wait_ge(s_proj, tile0 + (t + 1))
                        dve.wait_ge(s_lifted, FREE + b * 4 * BC + max(cc * 4 - 3 + t, 0))
                        nc.vector.tensor_scalar(clipped[:, t, :], ps[:, t % 2, :], cols_sb[:, 0:1], cols_sb[:, 1:2],
                                                ALU.max, ALU.min).then_inc(s_clipped, 1)

                    def part1(t):
                        dve.wait_ge(s_rest, tile0 + (t + 1))
                        nc.vector.tensor_copy(parts[:, t, 1, :], rest[:, t, :]).then_inc(s_p1, 1)

                    def part2(t):
                        dve.wait_ge(s_p1, tile0 + (t + 1))
                        nc.vector.tensor_tensor(parts[:, t, 2, :], rest[:, t, :], parts[:, t, 1, :],
                                                ALU.subtract).then_inc(s_p2, 1)

                    if cc + 1 < BC:
                        to_token(cc + 1)
                    dve.wait_ge(s_tr, FREE + b * 2 * BC + (cc * 2 + 2))
                    nc.vector.tensor_copy(vT[:, cc % 2, 1, :], ps[:, 5, :]).then_inc(s_trc[1], 1)
                    clip(0)
                    clip(1)
                    clip(2)
                    part1(0)
                    part2(0)
                    clip(3)
                    part1(1)
                    part2(1)
                    part1(2)
                    part2(2)
                    part1(3)
                    part2(3)

            def sum_groups(g, buf, loaded):
                dve.wait_ge(s_qk[buf], loaded)
                for n in range(2):
                    last = nc.vector.tensor_tensor(half_sums[:, n, :], kT[0:ROWS, buf, 2 * n * NG:(2 * n + 1) * NG],
                                                   kT[0:ROWS, buf, (2 * n + 1) * NG:(2 * n + 2) * NG], ALU.add)
                last.then_inc(s_half, 1)
                dve.wait_ge(s_half, g + 1)
                nc.vector.tensor_tensor(group_sums[:, buf, :], half_sums[:, 0, :], half_sums[:, 1, :],
                                        ALU.add).then_inc(s_gsum, 1)

            def max_groups(g, buf, n):
                dve.wait_ge(s_gps, g * (KB // 2) + (n + 1))
                nc.vector.tensor_reduce(group_max[:, buf, 2 * n:2 * n + 2], ps[:, 4:6, :], AX_X,
                                        ALU.max).then_inc(s_gmax, 1)

            def set_shift(g, buf):
                dve.wait_ge(s_shT, g + 1)
                nc.vector.tensor_scalar(shift_row[:, :], ps[0:KB, 4, 0:P], -1.0 / GROUP, -SHIFT * DH ** 0.5,
                                        ALU.mult, ALU.add).then_inc(s_shrow, 1)
                dve.wait_ge(s_shrow, g + 1)
                nc.vector.tensor_tensor(qT[ROWS:ROWS + KB, buf, :].rearrange("r (j q) -> r j q", j=KB),
                                        shift_row[:, :].unsqueeze(1).broadcast_to([KB, KB, P]),
                                        diag_sb[:, :].unsqueeze(2).broadcast_to([KB, KB, P]),
                                        ALU.mult).then_inc(s_shift, 1)

            def copy_out(g, buf):
                dve.wait_ge(s_pv, g * KB + KB)
                nc.vector.tensor_copy(oT[:, buf, :], ps[:, 6, :]).then_inc(s_oT, 1)

            def divide(g, buf):
                dve.wait_ge(s_otr, g + 1)
                tokens = ps[:, 7, :].rearrange("p (j c i) -> p j c i", j=CB, c=QC)
                nc.vector.reciprocal(rden[:, buf, :, :], tokens[:, :, :, DH:DH + 1].rearrange("p j c o -> p j (c o)")
                                     ).then_inc(s_rden, 1)
                dve.wait_ge(s_rden, g + 1)
                nc.vector.tensor_tensor(
                    o_heads[:, bass.ds(g, 1), :, :].rearrange("p g k i -> p (g k) i").rearrange(
                        "p (c j) i -> p j c i", j=CB),
                    tokens[:, :, :, 0:DH], rden[:, buf, :, :].unsqueeze(3).broadcast_to([P, CB, QC, DH]),
                    ALU.mult).then_inc(s_out, 1)

            def head(g, buf, first, last, loaded):
                if not first:
                    copy_out(g - 1, 1 - buf)
                    divide(g - 1, 1 - buf)
                if not last:
                    sum_groups(g + 1, 1 - buf, loaded)
                    for n in range(KB // 2):
                        max_groups(g + 1, 1 - buf, n)
                    set_shift(g + 1, 1 - buf)

            sum_groups(0, 0, 16 * LOADS)
            for n in range(KB // 2):
                max_groups(0, 0, n)
            set_shift(0, 0)
            head(0, 0, True, False, 16 * LOADS)
            with dve.Fori(0, HEADS // 2 - 1) as i:
                head(i * 2 + 1, 1, False, False, i * (16 * LOADS) + 2 * 16 * LOADS)
                head(i * 2 + 2, 0, False, False, i * (16 * LOADS) + 2 * 16 * LOADS)
            head(HEADS - 1, 1, False, True, 0)
            copy_out(HEADS - 1, 1)
            divide(HEADS - 1, 1)

            dve.wait_ge(s_out, HEADS)
            with dve.Fori(0, B) as b:
                def gather(cc):
                    dve.wait_ge(e_tr, FREE + b * 2 * BC + max(2 * (cc - 1), 0))
                    for j in range(CB):
                        last = nc.vector.tensor_copy(
                            token[:, cc % 2, j, :].rearrange("p (h i) -> p h i", h=H),
                            o_heads[:, bass.ds(b * H, H), cc * CB + j:cc * CB + j + 1, :].rearrange("p h k i -> p h (k i)"))
                    last.then_inc(e_token, 1)

                gather(0)
                for cc in range(BC):
                    if cc + 1 < BC:
                        gather(cc + 1)
                    dve.wait_ge(e_tr, FREE + b * 2 * BC + (cc * 2 + 2))
                    nc.vector.tensor_copy(vT[:, cc % 2, 1, :], ps[:, 5, :]).then_inc(e_trc[1], 1)
                    for n in range(2):
                        dve.wait_ge(e_wo, b * 2 * BC + (cc * 2 + n + 1))
                        nc.vector.tensor_copy(blocks(v_sb, b * KB + (cc * CB + n * 2), 2), ps[:, 6 + n, :]).then_inc(e_woc, 1)

            dve.wait_ge(s_acts, 5)
            link(nc.vector.tensor_scalar(s["u"], s["u"], 5.0, None, ALU.min))
            link(nc.vector.tensor_tensor(s["t"], s["u"], s["u"], ALU.mult))
            link(nc.vector.tensor_scalar(s["dn"], s["u"], EPS, None, ALU.add))
            link(nc.vector.reciprocal(s["dn"], s["dn"]))
            link(nc.vector.tensor_tensor(s["dn"], s["dn"], s["u"], ALU.mult))
            link(nc.vector.memset(s["a"], 1.0))
            for k in range(SINH_TERMS, 0, -1):
                link(nc.vector.scalar_tensor_tensor(s["a"], s["a"], 1.0 / (2 * k * (2 * k + 1)), s["t"],
                                                    ALU.mult, ALU.mult))
                link(nc.vector.tensor_scalar(s["a"], s["a"], 1.0, None, ALU.add))
            link(nc.vector.tensor_tensor(s["f"], s["a"], s["dn"], ALU.mult))
            with dve.Fori(0, CHUNKS) as c:
                for j in range(CB):
                    last = nc.vector.tensor_scalar(blocks(v_sb, c * CB + j), blocks(v_sb, c * CB + j),
                                                   sc["f"][:, bass.ds(c * CB + j, 1)], 8.0, ALU.mult, ALU.min)
                last.then_inc(e_scaled, 1)
                dve.wait_ge(e_scaled, c + 1)
                nc.vector.tensor_scalar(blocks(v_sb, c * CB, CB), blocks(v_sb, c * CB, CB), -8.0, None,
                                        ALU.max).then_inc(e_y, 1)
            dve.wait_ge(s_acts, 6)
            link(nc.vector.tensor_copy(v_sb[:, :, 0:1].rearrange("p n o -> p (n o)"), s["y0"]))

            with dve.Fori(0, CHUNKS) as c:
                layer_stats(v_sb, e_bn, c)
            dve.wait_ge(e_bn, CHUNKS)
            combine_stats()
            dve.wait_ge(s_acts, 7)
            link(nc.vector.reciprocal(s["rstd"], s["sd"]))
            with dve.Fori(0, CHUNKS) as c:
                normalise(lambda j: blocks(v_sb, c * CB + j), v_sb, lambda j: sc["mean"][:, bass.ds(c * CB + j, 1)], c).then_inc(e_x1, 1)
                dve.wait_ge(e_x1, c * 2 + 1)
                nc.vector.tensor_tensor(blocks(x_sb, c * CB, CB), blocks(x_sb, c * CB, CB),
                                        blocks(v_sb, c * CB, CB), ALU.add).then_inc(e_x1, 1)
                dve.wait_ge(e_x1, c * 2 + 2)
                layer_stats(x_sb, e_bn, c)
            dve.wait_ge(e_bn, 2 * CHUNKS)
            combine_stats()
            dve.wait_ge(s_acts, 8)
            link(nc.vector.reciprocal(s["rstd"], s["sd"]))

            with dve.Fori(0, B) as b:
                def prepare(cc):
                    par = cc % 2
                    c = b * BC + cc
                    dve.wait_ge(f_tr, FREE + b * 2 * BC + max(2 * (cc - 1), 0))
                    normalise(lambda j: token[:, par, j, :], x_sb,
                              lambda j: sc["mean"][:, bass.ds(c * CB + j, 1)], c).then_inc(f_token, 1)
                    if cc == 0:
                        nc.vector.memset(xT[:, par, :, 0:1], 0.0).then_inc(f_edge, 1)
                    else:
                        nc.vector.tensor_copy(xT[:, par, :, 0:1], xT[:, 1 - par, :, CT:CT + 1]).then_inc(f_edge, 1)
                    dve.wait_ge(f_tr, FREE + b * 2 * BC + (cc * 2 + 2))
                    nc.vector.tensor_copy(xT[:, par, 1, 1:CT + 1], ps[:, 5, :]).then_inc(f_trc[1], 1)
                    dve.wait_ge(f_trc[0], FREE + c + 1)
                    dve.wait_ge(f_trc[1], FREE + c + 1)
                    dve.wait_ge(f_edge, c + 1)
                    dve.wait_ge(f_r, FREE + b * BC + max(cc - 1, 0))
                    for w in range(2):
                        for k in range(KT):
                            last = nc.vector.tensor_scalar(mix_prev[:, par, w, k, :], xT[:, par, k, 0:CT],
                                                           omu_sb[:, w, k:k + 1], None, ALU.mult)
                        last.then_inc(f_prev, 1)
                        dve.wait_ge(f_prev, c * 2 + (w + 1))
                        for k in range(KT):
                            last = nc.vector.scalar_tensor_tensor(mixed[:, par, w, k, :], xT[:, par, k, 1:CT + 1],
                                                                  mu_sb[:, w, k:k + 1], mix_prev[:, par, w, k, :],
                                                                  ALU.mult, ALU.add)
                    last.then_inc(f_mix, 1)

                prepare(0)
                for cc in range(BC):
                    c = b * BC + cc
                    if cc + 1 < BC:
                        prepare(cc + 1)
                    dve.wait_ge(f_kv, FREE + b * 2 * BC + (cc * 2 + 2))
                    dve.wait_ge(f_sig, FREE + c + 1)
                    nc.vector.tensor_tensor(blocks(y_sb, c * CB, CB), vT[:, cc % 2, :, :].rearrange("p a b -> p (a b)"),
                                            ps[:, 6:8, :].rearrange("p a b -> p (a b)"), ALU.mult).then_inc(f_o, 1)
                    dve.wait_ge(f_o, FREE + c + 1)
                    layer_stats(y_sb, f_bn, c)
            dve.wait_ge(f_bn, CHUNKS)
            combine_stats()
            dve.wait_ge(s_acts, 9)
            link(nc.vector.reciprocal(s["rstd"], s["sd"]))
            with dve.Fori(0, CHUNKS) as c:
                normalise(lambda j: blocks(y_sb, c * CB + j), y_sb, lambda j: sc["mean"][:, bass.ds(c * CB + j, 1)], c).then_inc(e_x1, 1)
                dve.wait_ge(e_x1, c + (2 * CHUNKS + 1))
                nc.vector.tensor_tensor(blocks(y_sb, c * CB, CB), blocks(y_sb, c * CB, CB),
                                        blocks(x_sb, c * CB, CB), ALU.add).then_inc(f_out, 1)

        @block.tensor
        def _(pe):
            pe.wait_ge(s_const, 16 * N_CONST)

            def transposes(par, done):
                for k in range(KT):
                    for j in range(CB):
                        last = nc.tensor.transpose(ps[:, 4 + k, j * P:(j + 1) * P],
                                                   token[:, par, j, k * P:(k + 1) * P], ident_sb[:, :])
                    last.then_inc(done, 1)

            def by_token(bank, j, left, w):
                for k in range(KT):
                    last = nc.tensor.matmul(ps[:, bank, (j % 2) * D:(j % 2 + 1) * D], left[:, k, j * P:(j + 1) * P],
                                            w[:, k, :], start=(k == 0), stop=(k == KT - 1))
                return last

            def by_dim(bank, dt, w, right):
                for k in range(KT):
                    last = nc.tensor.matmul(ps[:, bank, :], w[:, k, dt * P:(dt + 1) * P], right[:, k, :],
                                            start=(k == 0), stop=(k == KT - 1))
                return last

            with pe.Fori(0, B) as b:
                for cc in range(BC):
                    par = cc % 2
                    c = b * BC + cc
                    tile0 = b * 4 * BC + cc * 4

                    def project(t):
                        pe.wait_ge(s_clipped, FREE + b * 4 * BC + max(cc * 4 + t - 1, 0))
                        by_dim(t % 2, t % 2, w_sb["q" if t < 2 else "k"], vT[:, par]).then_inc(s_proj, 1)

                    def norms(t):
                        pe.wait_ge(s_square, tile0 + (t + 1))
                        pe.wait_ge(s_root, FREE + b * 4 * BC + max(cc * 4 + t - 1, 0))
                        nc.tensor.matmul(ps[:, 2 + t % 2, :], headsum_sb[:, :], square[:, t, :], start=True,
                                         stop=True).then_inc(s_norm2, 1)

                    def values(n):
                        pe.wait_ge(s_vcopy, FREE + b * 2 * BC + max(cc * 2 + n - 1, 0))
                        for j in range(2):
                            last = by_token(6 + n, 2 * n + j, vT[:, par], w_sb["v"])
                        last.then_inc(s_vps, 1)

                    pe.wait_ge(s_token, c + 1)
                    pe.wait_ge(s_trc[0], FREE + c)
                    pe.wait_ge(s_trc[1], FREE + c)
                    transposes(par, s_tr)
                    pe.wait_ge(s_trc[0], FREE + c + 1)
                    pe.wait_ge(s_trc[1], FREE + c + 1)
                    project(0)
                    values(0)
                    project(1)
                    norms(0)
                    project(2)
                    norms(1)
                    values(1)
                    project(3)
                    norms(2)
                    norms(3)

            def scores(g, buf, kb, half, first):
                if not first or kb > 0:
                    pe.wait_ge(s_exp, g * (2 * KB) + (kb * 2 + half - 1))
                for n in range(2):
                    q0 = (half * 2 + n) * CT
                    last = nc.tensor.matmul(ps[:, half * 2 + n, :], kT[0:ROWS + KB, buf, kb * P:(kb + 1) * P],
                                            qT[0:ROWS + KB, buf, q0:q0 + CT], start=True, stop=True)
                last.then_inc(s_scores, 1)

            def weigh(g, buf, kb):
                pe.wait_ge(s_exp, g * (2 * KB) + (kb * 2 + 2))
                if kb == 0:
                    pe.wait_ge(s_vhead, g + 1)
                    pe.wait_ge(s_oT, g)
                for c in range(QC):
                    last = nc.tensor.matmul(ps[c * VW:(c + 1) * VW, 6, :], v_head[:, buf, kb, :],
                                            probs[:, kb % 4, c * CT:(c + 1) * CT], start=(kb == 0), stop=(kb == KB - 1))
                last.then_inc(s_pv, 1)

            def group_scores(g, buf, n):
                if n == 0:
                    pe.wait_ge(s_gsum, g + 1)
                    pe.wait_ge(s_shrow, g)
                pe.wait_ge(s_gmax, g * (KB // 2) + n)
                for j in range(2):
                    q0 = (2 * n + j) * P
                    last = nc.tensor.matmul(ps[:, 4 + j, :], qT[0:ROWS, buf, q0:q0 + P], group_sums[:, buf, :],
                                            start=True, stop=True)
                last.then_inc(s_gps, 1)

            def turn_max(g, buf):
                pe.wait_ge(s_gmax, g * (KB // 2) + KB // 2)
                nc.tensor.transpose(ps[0:KB, 4, 0:P], group_max[:, buf, :], ident_sb[:, :]).then_inc(s_shT, 1)

            def turn_out(g, buf):
                pe.wait_ge(s_oT, g + 1)
                pe.wait_ge(s_out, g)
                for j in range(CB):
                    last = nc.tensor.transpose(ps[:, 7, j * P:(j + 1) * P], oT[:, buf, j * P:(j + 1) * P], ident_sb[:, :])
                last.then_inc(s_otr, 1)

            def head(g, buf, first, last):
                for kb in range(KB):
                    if kb == 0:
                        pe.wait_ge(s_shift, g + 1)
                    scores(g, buf, kb, 0, first)
                    scores(g, buf, kb, 1, first)
                    if kb > 0:
                        weigh(g, buf, kb - 1)
                    elif not first:
                        weigh(g - 1, 1 - buf, KB - 1)
                    if kb == 1 and not first:
                        turn_out(g - 1, 1 - buf)
                    if 5 <= kb < 5 + KB // 2 and not last:
                        group_scores(g + 1, 1 - buf, kb - 5)
                    if kb == 14 and not last:
                        turn_max(g + 1, 1 - buf)

            pe.wait_ge(s_qk[0], 16 * LOADS)
            pe.wait_ge(s_trc[0], FREE + CHUNKS)
            pe.wait_ge(s_trc[1], FREE + CHUNKS)
            pe.wait_ge(s_clipped, FREE + 4 * CHUNKS)
            pe.wait_ge(s_root, FREE + 4 * CHUNKS)
            pe.wait_ge(s_vcopy, FREE + 2 * CHUNKS)
            for n in range(KB // 2):
                group_scores(0, 0, n)
            turn_max(0, 0)
            head(0, 0, True, False)
            with pe.Fori(0, HEADS // 2 - 1) as i:
                head(i * 2 + 1, 1, False, False)
                head(i * 2 + 2, 0, False, False)
            head(HEADS - 1, 1, False, True)
            weigh(HEADS - 1, 1, KB - 1)
            turn_out(HEADS - 1, 1)

            pe.wait_ge(s_out, HEADS)
            with pe.Fori(0, B) as b:
                for cc in range(BC):
                    c = b * BC + cc
                    pe.wait_ge(e_token, c + 1)
                    pe.wait_ge(e_trc[0], FREE + c)
                    pe.wait_ge(e_trc[1], FREE + c)
                    transposes(cc % 2, e_tr)
                    pe.wait_ge(e_trc[0], FREE + c + 1)
                    pe.wait_ge(e_trc[1], FREE + c + 1)
                    for n in range(2):
                        pe.wait_ge(e_woc, FREE + b * 2 * BC + max(cc * 2 + n - 1, 0))
                        for j in range(2):
                            last = by_token(6 + n, 2 * n + j, vT[:, cc % 2], w_sb["o"])
                        last.then_inc(e_wo, 1)

            pe.wait_ge(e_woc, FREE + 2 * CHUNKS)
            with pe.Fori(0, B) as b:
                def turn(cc):
                    c = b * BC + cc
                    pe.wait_ge(f_token, c + 1)
                    pe.wait_ge(f_trc[0], FREE + c)
                    pe.wait_ge(f_trc[1], FREE + c)
                    transposes(cc % 2, f_tr)

                turn(0)
                for cc in range(BC):
                    par = cc % 2
                    c = b * BC + cc
                    pe.wait_ge(f_mix, FREE + c + 1)
                    for dt in range(KT):
                        pe.wait_ge(f_relu, FREE + c * KT)
                        by_dim(2 + dt, dt, w_sb["kf"], mixed[:, par, 1]).then_inc(f_k, 1)
                    if cc + 1 < BC:
                        turn(cc + 1)
                    pe.wait_ge(f_sig, FREE + c)
                    for j in range(CB):
                        last = by_token(j // 2, j, mixed[:, par, 0], w_sb["r"])
                    last.then_inc(f_r, 1)
                    pe.wait_ge(f_sq, FREE + c * KT + KT)
                    pe.wait_ge(f_o, FREE + c)
                    for n in range(2):
                        for j in range(2):
                            last = by_token(6 + n, 2 * n + j, square[:, 2:4], w_sb["vf"])
                        last.then_inc(f_kv, 1)


def kernel(L0_attn_x, L0_attn_Wq, L0_attn_Wk, L0_attn_Wv, L0_attn_Wo, L0_ffn_W_r, L0_ffn_W_k, L0_ffn_W_v,
           L0_ffn_mu_r, L0_ffn_mu_k):
    import numpy as np
    import concourse.bacc as bacc
    from concourse.bass_utils import run_bass_kernel_spmd

    ident = np.eye(P, dtype=np.float32)
    dim0 = np.arange(P) % DH == 0
    head_of = np.arange(P) // DH
    headsum = ((head_of[:, None] == head_of[None, :]) & dim0[None, :]).astype(np.float32)
    cols = np.zeros((P, 4), np.float32)
    cols[:, 0] = np.where(dim0, 0.0, -5.0)
    cols[:, 1] = np.where(dim0, 0.0, 5.0)
    cols[:, 2] = np.where(dim0, 1.0 + EPS, 0.0)
    arrays = {
        "x": np.ascontiguousarray(L0_attn_x).reshape(B * T, D),
        "wq": np.ascontiguousarray(np.asarray(L0_attn_Wq).T),
        "wk": np.ascontiguousarray(np.asarray(L0_attn_Wk).T),
        "wv": np.ascontiguousarray(np.asarray(L0_attn_Wv).T),
        "wo": np.ascontiguousarray(np.asarray(L0_attn_Wo).T),
        "wr": np.ascontiguousarray(np.asarray(L0_ffn_W_r).T),
        "wkf": np.ascontiguousarray(np.asarray(L0_ffn_W_k).T),
        "wvf": np.ascontiguousarray(np.asarray(L0_ffn_W_v).T),
        "mus": np.ascontiguousarray(np.stack([np.asarray(m).reshape(KT, P).T for m in (L0_ffn_mu_r, L0_ffn_mu_k)], 1)),
        "ident": ident, "headsum": headsum, "cols": cols, "diag": np.eye(KB, dtype=np.float32),
    }
    nc = bacc.Bacc("TRN2", target_bir_lowering=False, num_devices=1)
    args = [nc.dram_tensor(f"in_{n}", a.shape, mybir.dt.from_np(a.dtype), kind="ExternalInput").ap()
            for n, a in arrays.items()]
    args.append(nc.dram_tensor("out_0", (B * T, D), F32, kind="ExternalOutput").ap())
    sandwich(nc, *args)
    r = run_bass_kernel_spmd(nc, [{f"in_{n}": a for n, a in arrays.items()}], core_ids=[0])
    return r.results[0]["out_0"].reshape(B, T, D)
```

```python
from contextlib import ExitStack
from math import factorial

import concourse.bass as bass
from concourse import mybir

P = 128
F32 = mybir.dt.float32
BF16 = mybir.dt.bfloat16
ACT = mybir.ActivationFunctionType
ALU = mybir.AluOpType
AX_X = mybir.AxisListType.X

B, T, D, H = 2, 2048, 256, 16
DH = D // H
HEADS = B * H
BLOCKS = B * T // P
KB = T // P
CB = 4
BC = KB // CB
CHUNKS = B * BC
CT = CB * P
KT = D // P
PARTS = 3
PAIRS = ((0, 0), (0, 1), (0, 2), (1, 0), (1, 1), (2, 0))
ROWS = len(PAIRS) * DH
GROUP = 4
NG = T // GROUP
VW = 32
QC = T // CT
EPS = 1e-6
LN_EPS = 1e-5
SHIFT = 65.0
SINH_TERMS = 14
SR = (DH - 1) * H // 2
LOADS = PARTS
G_FIRST, G_STEPS = 2, 11
OUT_ROOT = 9
NORM_STEPS = {(n // 4, n % 4): (BC + c, part) for n, (c, part) in enumerate((
    (0, "stats"), (1, "stats"), (0, 0), (0, 1), (2, "stats"), (1, 0), (1, 1), (3, "stats"), (2, 0), (2, 1),
    (3, 0), (3, 1)))}
GROUPS_AT = {(BC + 1 + j // 6, j % 6): (j,) for j in range(KB)}


def sandwich(nc, x, wq, wk, wv, wo, wr, wkf, wvf, mus, ident, headsum, sign, diag, out):
    with ExitStack() as ctx:
        def sb(name, shape, dt=F32):
            return ctx.enter_context(nc.sbuf_tensor(name, shape, dt))

        def sem(name):
            return ctx.enter_context(nc.semaphore(name))

        q_parts = nc.dram_tensor("q_parts", (PARTS, B, DH, H, T), BF16, kind="Internal").ap()
        k_parts = nc.dram_tensor("k_parts", (PARTS, B, DH, H, T), BF16, kind="Internal").ap()

        w_sb = {n: sb(f"w_{n}", [P, KT, 2 * SR if n in "qk" else D]) for n in ("q", "k", "v", "o", "r", "kf", "vf")}
        ident_sb = sb("ident_sb", [P, P])
        headsum_sb = sb("headsum_sb", [SR, 2, VW])
        sign_sb = sb("sign_sb", [2 * VW, 1])
        diag_sb = sb("diag_sb", [KB, KB])
        mu_sb = sb("mu_sb", [P, 2, KT])
        omu_sb = sb("omu_sb", [P, 2, KT])
        one_eps = sb("one_eps", [P, 1])
        ln_eps = sb("ln_eps", [P, 1])
        eps_col = sb("eps_col", [P, 1])
        one_col = sb("one_col", [P, 1])
        zero_col = sb("zero_col", [P, KT])

        x_sb = sb("x_sb", [P, BLOCKS, D])
        y_sb = sb("y_sb", [P, BLOCKS, D])
        v_sb = sb("v_sb", [P, BLOCKS, D])
        by_head = "p (g k i) -> p g k i"
        v_heads = v_sb[:, :, :].rearrange("p a b -> p (a b)").rearrange(by_head, g=HEADS, k=KB)
        o_heads = y_sb[:, :, :].rearrange("p a b -> p (a b)").rearrange(by_head, g=HEADS, k=KB)

        work = sb("work", [P, 4 * T])
        clipped, rest = (work[:, n * T:(n + 1) * T].rearrange("p (t n) -> p t n", t=4) for n in range(2))
        root, dim0 = (work[0:2 * VW, (4 + n) * T // 2:(5 + n) * T // 2].rearrange("p (b n) -> p b n", b=2)
                      for n in range(2))
        parts0 = work[0:2 * VW, 3 * T:3 * T + PARTS * CT].bitcast(BF16).rearrange("p (b s n) -> p b s n", b=2, s=PARTS)
        probs = work[:, :].rearrange("p (n q) -> p n q", n=4)
        xT = work[:, 0:2 * KT * (CT + 1)].rearrange("p (b k t) -> p b k t", b=2, k=KT)
        mixed = work[:, T + 16:3 * T + 16].rearrange("p (b w k t) -> p b w k t", b=2, w=2, k=KT)
        mix_prev = v_sb[:, :, :].rearrange("p a b -> p (a b)")[:, 0:4 * KT * CT].rearrange(
            "p (b w k t) -> p b w k t", b=2, w=2, k=KT)
        token = sb("token", [P, 2, CB, D])
        vT = sb("vT", [P, 2, KT, CT])
        square = sb("square", [P, 4, CT])
        unread = sb("unread", [P, 2, D])
        parts = sb("parts", [P, 4, PARTS, CT], BF16)

        qT = sb("qT", [P, 2, T], BF16)
        kT = sb("kT", [P, 2, T], BF16)
        half_sums = unread[0:ROWS, :, :].rearrange("p a b -> p (a b)").bitcast(BF16).rearrange("p (n k) -> p n k", n=2)
        group_sums = sb("group_sums", [ROWS, 2, NG], BF16)
        v_head = sb("v_head", [P, 2, KB, VW])
        group_max = sb("group_max", [P, 2, KB])
        shift_row = sb("shift_row", [KB, P])
        oT = square[:, 0:2, :]
        rden = sb("rden", [P, 2, CB, QC])

        stats = sb("stats", [P, BLOCKS, 6])
        sc = {n: sb(f"sc_{n}", [P, BLOCKS]) for n in
              ("sd", "rstd", "ss", "y0", "z", "zm", "t", "u", "w", "d", "d0", "inn", "f", "a", "dn", "mean", "var", "m2", "lo", "hi", "shift", "scale")}

        ps = ctx.enter_context(nc.psum_tensor("ps", [P, 8, CT], F32))

        s_const = sem("s_const")
        s_memset = sem("s_memset")
        s_omu = sem("s_omu")
        s_x = [sem(f"s_x{c}") for c in range(CHUNKS)]
        s_bn, s_var, s_sd, s_norm, s_clip, s_ss = map(sem, ("s_bn", "s_var", "s_sd", "s_norm", "s_clip", "s_ss"))
        s_link = sem("s_link")
        s_ask = sem("s_ask")
        s_answer = sem("s_answer")
        s_token, s_tr, s_vT = map(sem, ("s_token", "s_tr", "s_vT"))
        s_vps, s_vcopy = map(sem, ("s_vps", "s_vcopy"))
        s_proj, s_clipped, s_square, s_p0, s_rest, s_p1, s_p2 = map(
            sem, ("s_proj", "s_clipped", "s_square", "s_p0", "s_rest", "s_p1", "s_p2"))
        s_norms, s_root, s_dim0, s_z0, s_zrest, s_z1, s_z2 = map(
            sem, ("s_norms", "s_root", "s_dim0", "s_z0", "s_zrest", "s_z1", "s_z2"))
        s_store = [sem(f"s_store{n}") for n in range(4)]
        s_store0 = [sem(f"s_store0_{n}") for n in range(2)]
        s_q = [sem("s_q0"), sem("s_q1")]
        s_k = [sem("s_k0"), sem("s_k1")]
        s_half, s_gsum, s_vhead, s_gps, s_gmax, s_shT, s_shrow, s_shift = map(
            sem, ("s_half", "s_gsum", "s_vhead", "s_gps", "s_gmax", "s_shT", "s_shrow", "s_shift"))
        s_scores, s_exp, s_pv, s_oT, s_otr, s_rden, s_out = map(
            sem, ("s_scores", "s_exp", "s_pv", "s_oT", "s_otr", "s_rden", "s_out"))
        e_token, e_tr, e_trc, e_wo, e_woc, e_ss = map(sem, ("e_token", "e_tr", "e_trc", "e_wo", "e_woc", "e_ss"))
        e_bn0, e_clip, e_bn, e_norm, e_x1, e_bn1 = map(sem, ("e_bn0", "e_clip", "e_bn", "e_norm", "e_x1", "e_bn1"))
        f_token, f_tr, f_xT, f_prev, f_mix, f_k, f_relu, f_sq = map(
            sem, ("f_token", "f_tr", "f_xT", "f_prev", "f_mix", "f_k", "f_relu", "f_sq"))
        f_r, f_sig, f_kv, f_o, f_bn, f_norm = map(sem, ("f_r", "f_sig", "f_kv", "f_o", "f_bn", "f_norm"))
        f_out = [sem("f_out0"), sem("f_out1")]
        s_done = sem("s_done")

        N_CONST = 5 + len(w_sb)
        x_blocks = x.rearrange("(n p) d -> p n d", p=P)
        out_blocks = out.rearrange("(n p) d -> p n d", p=P)

        def blocks(t, first, n=1):
            return t[:, bass.ds(first, n), :].rearrange("p n d -> p (n d)")

        def after(eng, semaphore, value):
            if not isinstance(value, int) or value > 0:
                eng.wait_ge(semaphore, value)

        block = ctx.enter_context(nc.Block())

        @block.sync
        def _(sp):
            for c in range(CHUNKS):
                sp.dma_start(x_sb[:, c * CB:(c + 1) * CB, :], x_blocks[:, c * CB:(c + 1) * CB, :]).then_inc(s_x[c], 16)
            for t, a in ((ident_sb[:, :], ident), (headsum_sb[:, :, :], headsum), (sign_sb[:, :], sign),
                         (diag_sb[:, :], diag)):
                sp.dma_start(t, a).then_inc(s_const, 16)
            sp.dma_start(mu_sb[:, :, :], mus).then_inc(s_const, 16)
            for n, a in (("q", wq), ("k", wk), ("v", wv), ("o", wo), ("r", wr), ("kf", wkf), ("vf", wvf)):
                sp.dma_start(w_sb[n][:, :, :], a.rearrange("(k p) d -> p k d", p=P)).then_inc(s_const, 16)

            def store0(c):
                b, cc = c // BC, c % BC
                sp.wait_ge(s_z0, c + 1)
                sp.wait_ge(s_z1, c + 1)
                sp.wait_ge(s_z2, c + 1)
                for n, dst in enumerate((q_parts, k_parts)):
                    sp.dma_start(dst[:, b, 0, :, cc * CT:(cc + 1) * CT].rearrange("s h t -> h s t"),
                                 parts0[n * VW:n * VW + H, c % 2, :, :]).then_inc(s_store0[c % 2], 16)

            def load_head(b, h, buf):
                runs = [(p, PARTS - p, PAIRS.index((p, 0)) * DH) for p in range(PARTS)]
                for p, n, row in runs:
                    sp.dma_start(kT[row:row + n * DH, buf, :],
                                 k_parts[0:n, b, :, bass.ds(h, 1), :].rearrange("s i h t -> s i (h t)")
                                 ).then_inc(s_k[buf], 16)
                for p, n, row in runs:
                    sp.dma_start(qT[row:row + n * DH, buf, :],
                                 q_parts[p:p + 1, b, :, bass.ds(h, 1), :].rearrange("s i h t -> s i (h t)")
                                 .broadcast_to([n, DH, T])).then_inc(s_q[buf], 16)

            def batch_stored(b):
                for t in range(4):
                    sp.wait_ge(s_store[t], 16 * (BC * (b + 1) + (b == 0 and t < 2)))
                for n in range(2):
                    sp.wait_ge(s_store0[n], 32 * BC // 2 * (b + 1))

            for c in range(CHUNKS):
                b, cc = c // BC, c % BC
                for t in range(4):
                    rows = (q_parts, k_parts)[t // 2][:, b, :, :, :].rearrange("s i h t -> (i h) s t")
                    sp.wait_ge(s_p0, c * 4 + t + 1)
                    sp.wait_ge(s_p1, c * 4 + t + 1)
                    sp.wait_ge(s_p2, c * 4 + t + 1)
                    sp.dma_start(rows[H + (t % 2) * SR:H + (t % 2 + 1) * SR, :, cc * CT:(cc + 1) * CT],
                                 parts[0:SR, t, :, :]).then_inc(s_store[t], 16)
                    if t == 1 and c > 0:
                        store0(c - 1)
                    if t == 1 and c == BC:
                        batch_stored(0)
                        load_head(0, 0, 0)
                        load_head(0, 1, 1)
            store0(CHUNKS - 1)
            for b in range(B):
                if b == 1:
                    batch_stored(1)
                with sp.Fori(1 - b, H // 2) as i:
                    for buf in range(2):
                        sp.wait_ge(s_scores, i * (4 * KB) + (b * H + buf - 1) * 2 * KB)
                        load_head(b, i * 2 + buf, buf)
            for c in range(CHUNKS):
                sp.wait_ge(f_out[c // BC], c % BC + 1)
                sp.dma_start(out_blocks[:, c * CB:(c + 1) * CB, :],
                             y_sb[:, c * CB:(c + 1) * CB, :]).then_inc(s_done, 16)
            sp.wait_ge(s_done, 16 * CHUNKS)

        @block.gpsimd
        def _(pool):
            nc.gpsimd.memset(one_eps[:, :], 1.0 + EPS).then_inc(s_memset, 1)
            nc.gpsimd.memset(ln_eps[:, :], LN_EPS).then_inc(s_memset, 1)
            nc.gpsimd.memset(eps_col[:, :], EPS).then_inc(s_memset, 1)
            nc.gpsimd.memset(one_col[:, :], 1.0).then_inc(s_memset, 1)
            nc.gpsimd.memset(zero_col[:, :], 0.0).then_inc(s_memset, 1)
            nc.gpsimd.memset(v_head[:, :, :, DH + 1:VW], 0.0).then_inc(s_memset, 1)
            nc.gpsimd.memset(v_head[:, :, :, DH:DH + 1], 1.0).then_inc(s_memset, 1)

            pool.wait_ge(s_memset, 7)
            nc.gpsimd.memset(kT[ROWS:ROWS + KB, :, :], 1.0).then_inc(s_memset, 1)
            pool.wait_ge(s_memset, 8)

            def second_rest(c):
                pool.wait_ge(s_z0, c + 1)
                nc.gpsimd.tensor_tensor(dim0[:, c % 2, :], dim0[:, c % 2, :], parts0[:, c % 2, 0, :],
                                        ALU.subtract).then_inc(s_zrest, 1)

            def load_v(g, buf):
                v = v_heads[:, bass.ds(g, 1), :, :].rearrange("p g k i -> p (g k) i")
                nc.gpsimd.tensor_tensor(v_head[:, buf, :, 0:DH], v, one_col[:, :].unsqueeze(2).broadcast_to([P, KB, DH]),
                                        ALU.mult).then_inc(s_vhead, 1)

            for c in range(CHUNKS):
                for t in range(4):
                    pool.wait_ge(s_p0, c * 4 + t + 1)
                    after(pool, s_p2, (c - 1) * 4 + t + 1)
                    nc.gpsimd.tensor_tensor(rest[0:SR, t, :], clipped[0:SR, t, :], parts[0:SR, t, 0, :],
                                            ALU.subtract).then_inc(s_rest, 1)
                    if t == 1 and c > 0:
                        second_rest(c - 1)
                if c == BC:
                    pool.wait_ge(s_vcopy, 2 * BC)
                    load_v(0, 0)
                    load_v(1, 1)
            second_rest(CHUNKS - 1)

            pool.wait_ge(s_vcopy, 2 * CHUNKS)
            with pool.Fori(1, HEADS // 2) as i:
                for buf in range(2):
                    pool.wait_ge(s_pv, i * (2 * KB) + (buf - 1) * KB)
                    load_v(i * 2 + buf, buf)

            for c in range(CHUNKS):
                b, cc = c // BC, c % BC
                if cc == 0:
                    pool.wait_ge(s_out, (b + 1) * H)
                after(pool, e_tr, c - 1)
                for j in range(CB):
                    last = nc.gpsimd.tensor_tensor(
                        token[:, c % 2, j, :].rearrange("p (h i) -> p h i", h=H),
                        o_heads[:, b * H:(b + 1) * H, cc * CB + j, :],
                        one_col[:, :].unsqueeze(2).broadcast_to([P, H, DH]), ALU.mult)
                last.then_inc(e_token, 1)

            def residual(c):
                pool.wait_ge(e_norm, c + 1)
                nc.gpsimd.tensor_tensor(blocks(x_sb, c * CB, CB), blocks(x_sb, c * CB, CB),
                                        blocks(v_sb, c * CB, CB), ALU.add).then_inc(e_x1, 1)

            for c in range(CHUNKS):
                residual(c)

            for c in range(BC):
                pool.wait_ge(f_norm, c + 1)
                nc.gpsimd.tensor_tensor(blocks(y_sb, c * CB, CB), blocks(y_sb, c * CB, CB),
                                        blocks(x_sb, c * CB, CB), ALU.add).then_inc(f_out[0], 1)

        @block.scalar
        def _(act):
            act.wait_ge(s_memset, 8)

            def row_norms(src, done, c, first=0):
                for j in range(CB):
                    blk = c * CB + j
                    after(act, done, blk - first - 1)
                    nc.scalar.activation(unread[:, blk % 2, 1:D], src[:, blk, 1:D], ACT.Square,
                                         accum_out=sc["ss"][:, blk:blk + 1]).then_inc(done, 1)

            asked = [0]

            def answer(dst, src, func, b, bias=None, own=None, n=KB):
                if own:
                    act.wait_ge(*own)
                else:
                    asked[0] += 1
                    act.wait_ge(s_ask, asked[0])
                nc.scalar.activation(sc[dst][:, b * n:(b + 1) * n], sc[src][:, b * n:(b + 1) * n], func,
                                     **({} if bias is None else {"bias": bias[:, 0:1]})).then_inc(s_answer, 1)

            def norm_sd(c):
                act.wait_ge(s_var, c + 1)
                nc.scalar.activation(sc["sd"][:, c * CB:(c + 1) * CB], sc["var"][:, c * CB:(c + 1) * CB], ACT.Sqrt,
                                     bias=ln_eps[:, 0:1]).then_inc(s_sd, 1)

            def norm_squares(c):
                act.wait_ge(s_clip, c + 1)
                row_norms(y_sb, s_ss, c)

            def log_map(b, stage):
                if stage == 0:
                    answer("y0", "ss", ACT.Sqrt, b, one_eps, own=(s_ss, (b + 1) * KB))
                if stage == 1:
                    answer("u", "t", ACT.Sqrt, b)
                    answer("dn", "inn", ACT.Sqrt, b)
                if stage == 2:
                    answer("d", "w", ACT.Ln, b)

            norm_sd(0)
            for c in range(BC):
                if c + 1 < BC:
                    norm_sd(c + 1)
                norm_squares(c)
            for stage in range(3):
                log_map(0, stage)

            act.wait_ge(s_const, 16 * N_CONST)

            def make_square(c, t):
                act.wait_ge(s_clipped, c * 4 + t + 1)
                after(act, s_norms, c)
                nc.scalar.activation(square[0:SR, t, :], clipped[0:SR, t, :], ACT.Square).then_inc(s_square, 1)

            def part0(c, t):
                after(act, s_store[t], 16 * c)
                nc.scalar.activation(parts[0:SR, t, 0, :], clipped[0:SR, t, :], ACT.Copy).then_inc(s_p0, 1)

            def v_copy(c, n):
                b, cc = c // BC, c % BC
                act.wait_ge(s_vps, c * 2 + n + 1)
                for j in range(2):
                    last = nc.scalar.activation(v_heads[:, b * H:(b + 1) * H, cc * CB + n * 2 + j, :],
                                                ps[:, 6 + n, j * D:(j + 1) * D].rearrange("p (h i) -> p h i", h=H),
                                                ACT.Copy)
                last.then_inc(s_vcopy, 1)

            def make_root(c):
                act.wait_ge(s_norms, c + 1)
                after(act, s_dim0, c - 1)
                nc.scalar.activation(root[:, c % 2, :], ps[0:2 * VW, 2, :], ACT.Sqrt,
                                     bias=one_eps[0:2 * VW, 0:1]).then_inc(s_root, 1)

            def part00(c):
                act.wait_ge(s_dim0, c + 1)
                after(act, s_store0[c % 2], 32 * (c // 2))
                nc.scalar.activation(parts0[:, c % 2, 0, :], dim0[:, c % 2, :], ACT.Copy).then_inc(s_z0, 1)

            for c in range(CHUNKS):
                act.wait_ge(s_tr, c + 1)
                nc.scalar.activation(vT[:, c % 2, :, :], ps[:, 4:6, :], ACT.Copy).then_inc(s_vT, 1)
                make_square(c, 0)
                part0(c, 0)
                if c > 0:
                    make_root(c - 1)
                if c == 2:
                    norm_sd(BC + 3)
                    norm_squares(BC + 1)
                if c == BC - 1:
                    norm_squares(BC + 3)
                    log_map(1, 0)
                make_square(c, 1)
                part0(c, 1)
                if c == 0:
                    norm_sd(BC)
                if c == 1:
                    norm_squares(BC)
                if c == BC - 1:
                    log_map(1, 1)
                v_copy(c, 0)
                if c > 0:
                    part00(c - 1)
                make_square(c, 2)
                part0(c, 2)
                if c == 0:
                    norm_sd(BC + 1)
                if c == 1:
                    norm_sd(BC + 2)
                if c == 2:
                    norm_squares(BC + 2)
                if c == BC - 1:
                    log_map(1, 2)
                v_copy(c, 1)
                make_square(c, 3)
                part0(c, 3)
            make_root(CHUNKS - 1)
            part00(CHUNKS - 1)

            def exp_map(b):
                answer("u", "ss", ACT.Sqrt, b, eps_col, own=(e_ss, KB) if b == 1 else None)

            def exps(g, first, last=False):
                for kb in range(KB):
                    if last and kb == OUT_ROOT:
                        exp_map(0)
                    if first and kb == 0:
                        act.wait_ge(s_rest, 4 * CHUNKS)
                        act.wait_ge(s_square, 4 * CHUNKS)
                    if first and kb == 1:
                        act.wait_ge(s_p2, 4 * CHUNKS)
                    if first and kb == 2:
                        act.wait_ge(s_z2, CHUNKS)
                    if first and kb == 3:
                        for n in range(2):
                            act.wait_ge(s_store0[n], 32 * CHUNKS // 2)
                    for half in range(2):
                        act.wait_ge(s_scores, g * (2 * KB) + (kb * 2 + half + 1))
                        if not first or kb >= 4:
                            act.wait_ge(s_pv, g * KB + (kb - 3))
                        nc.scalar.activation(
                            probs[:, kb % 4, half * 2 * CT:(half + 1) * 2 * CT].rearrange("p (a q) -> p a q", a=2),
                            ps[:, half * 2:half * 2 + 2, :], ACT.Exp, scale=DH ** -0.5).then_inc(s_exp, 1)

            exps(0, True)
            with act.Fori(0, HEADS // 2 - 1) as i:
                exps(i * 2 + 1, False)
                exps(i * 2 + 2, False)
            exps(HEADS - 1, False, True)

            def out_vT(c):
                act.wait_ge(e_tr, c + 1)
                after(act, e_wo, 2 * (c - 1))
                nc.scalar.activation(vT[:, c % 2, :, :], ps[:, 4:6, :], ACT.Copy).then_inc(e_trc, 1)

            def out(c):
                if c + 1 < CHUNKS:
                    out_vT(c + 1)
                for n in range(2):
                    act.wait_ge(e_wo, c * 2 + n + 1)
                    nc.scalar.activation(blocks(v_sb, c * CB + n * 2, 2), ps[:, 6 + n, :], ACT.Copy).then_inc(e_woc, 1)
                act.wait_ge(e_woc, c * 2 + 2)
                row_norms(v_sb, e_ss, c, KB)

            def out_norm(b):
                answer("y0", "inn", ACT.Sqrt, b, one_eps)
                answer("sd", "var", ACT.Sqrt, b, ln_eps)

            def token_norm(b, n=KB):
                answer("sd", "var", ACT.Sqrt, b, ln_eps, n=n)

            def to_xT(c):
                par = c % 2
                act.wait_ge(f_tr, c + 1)
                after(act, f_mix, 2 * (c - 1))
                if c:
                    act.wait_ge(f_xT, 2 * c)
                nc.scalar.activation(xT[:, par, :, 0], zero_col[:, :] if c % BC == 0 else xT[:, 1 - par, :, CT],
                                     ACT.Copy).then_inc(f_xT, 1)
                nc.scalar.activation(xT[:, par, :, 1:CT + 1], ps[:, 4:6, :], ACT.Copy).then_inc(f_xT, 1)
                act.wait_ge(f_xT, 2 * c + 2)
                for w in range(2):
                    for k in range(KT):
                        last = nc.scalar.activation(mix_prev[:, par, w, k, :], xT[:, par, k, 0:CT], ACT.Copy,
                                                    scale=omu_sb[:, w, k:k + 1])
                    last.then_inc(f_prev, 1)

            def relu_squares(c):
                after(act, f_sq, c * KT)
                for dt in range(KT):
                    act.wait_ge(f_k, c * KT + dt + 1)
                    nc.scalar.activation(square[:, dt, :], ps[:, 2 + dt, :], ACT.Relu).then_inc(f_relu, 1)
                after(act, f_kv, c * 2)
                for dt in range(KT):
                    act.wait_ge(f_relu, c * KT + dt + 1)
                    nc.scalar.activation(square[:, 2 + dt, :], square[:, dt, :], ACT.Square).then_inc(f_sq, 1)

            def gate(c):
                act.wait_ge(f_r, c + 1)
                after(act, f_o, c - 1)
                nc.scalar.activation(vT[:, c % 2, :, :], ps[:, 0:2, :], ACT.Sigmoid).then_inc(f_sig, 1)

            out_norm(0)
            out_vT(BC)
            out(BC)
            out(BC + 1)
            out(BC + 2)
            token_norm(0)
            out(BC + 3)
            to_xT(0)
            exp_map(1)
            for c in range(CHUNKS):
                if c + 1 < CHUNKS:
                    to_xT(c + 1)
                relu_squares(c)
                if c == BC + 1:
                    token_norm(0)
                gate(c)
                if c == 1:
                    out_norm(1)
                if c == 2:
                    token_norm(1)
                if c == BC + 2:
                    token_norm(2, 2 * CB)
                if c == BC + 3:
                    token_norm(CHUNKS - 2, CB)
            token_norm(CHUNKS - 1, CB)

        @block.vector
        def _(dve):
            links = [0]

            def link(ins):
                links[0] += 1
                ins.then_inc(s_link, 1)
                dve.wait_ge(s_link, links[0])

            def small(name, b, n=KB):
                return sc[name][:, b * n:(b + 1) * n]

            def layer_stats(src, done, c, first=0):
                for j in range(CB):
                    last = nc.vector.bn_stats(stats[:, c * CB + j, :], src[:, c * CB + j, first:D])
                last.then_inc(done, 1)

            def statistic(n, b, size):
                return stats[:, b * size:(b + 1) * size, n:n + 1].rearrange("p n o -> p (n o)")

            def combine_stats(b, size=KB):
                even, odd, m2_even, m2_odd = (statistic(n, b, size) for n in (1, 4, 2, 5))
                a, w, z, mean = (small(n, b, size) for n in ("a", "w", "z", "mean"))
                nc.vector.tensor_tensor(a, even, odd, ALU.subtract)
                nc.vector.tensor_tensor(w, m2_even, m2_odd, ALU.add)
                link(nc.vector.tensor_tensor(z, even, odd, ALU.add))
                nc.vector.tensor_scalar(mean, z, 0.5, None, ALU.mult)
                link(nc.vector.scalar_tensor_tensor(a, a, 0.25, a, ALU.mult, ALU.mult))
                return nc.vector.scalar_tensor_tensor(small("var", b, size), w, 1.0 / D, a, ALU.mult, ALU.add)

            answers = [0]

            def ask(ins):
                ins.then_inc(s_ask, 1)

            def wait_answer():
                answers[0] += 1
                dve.wait_ge(s_answer, answers[0])

            dve.wait_ge(s_memset, 8)

            def norm_stats(c):
                dve.wait_ge(s_x[c], 16)
                layer_stats(x_sb, s_bn, c)
                dve.wait_ge(s_bn, c + 1)
                combine_stats(c, CB).then_inc(s_var, 1)

            def norm(c, half=None):
                if half != 1:
                    dve.wait_ge(s_sd, c + 1)
                    link(nc.vector.reciprocal(small("rstd", c, CB), small("sd", c, CB)))
                for j in range(0 if half != 1 else CB // 2, CB if half != 0 else CB // 2):
                    blk = c * CB + j
                    last = nc.vector.tensor_scalar(y_sb[:, blk, :], x_sb[:, blk, :], sc["mean"][:, blk:blk + 1],
                                                   sc["rstd"][:, blk:blk + 1], ALU.subtract, ALU.mult)
                if half == 0:
                    return
                last.then_inc(s_norm, 1)
                dve.wait_ge(s_norm, c + 1)
                nc.vector.tensor_scalar(blocks(y_sb, c * CB, CB), blocks(y_sb, c * CB, CB),
                                        8.0, -8.0, ALU.min, ALU.max).then_inc(s_clip, 1)

            def log_map(b, stage):
                s = {n: small(n, b) for n in sc}
                if stage == 1:
                    wait_answer()
                    ask(nc.vector.tensor_tensor(s["w"], s["z"], s["u"], ALU.add))
                    link(nc.vector.tensor_copy(y_sb[:, b * KB:(b + 1) * KB, 0:1].rearrange("p n o -> p (n o)"), s["d0"]))
                    wait_answer()
                    link(nc.vector.tensor_scalar(s["dn"], s["dn"], EPS, None, ALU.add))
                    link(nc.vector.reciprocal(s["dn"], s["dn"]))
                if stage == 2:
                    wait_answer()
                    link(nc.vector.scalar_tensor_tensor(s["f"], s["d"], 0.001, s["dn"], ALU.max, ALU.mult))
                if stage > 0:
                    return
                wait_answer()
                link(nc.vector.tensor_scalar(s["z"], s["y0"], 1.0 + EPS, None, ALU.max))
                link(nc.vector.tensor_scalar(s["dn"], s["z"], -1.0, None, ALU.add))
                ask(nc.vector.scalar_tensor_tensor(s["t"], s["z"], 1.0, s["dn"], ALU.add, ALU.mult))
                link(nc.vector.tensor_tensor(s["d0"], s["y0"], s["z"], ALU.subtract))
                link(nc.vector.tensor_tensor(s["a"], s["d0"], s["d0"], ALU.mult))
                link(nc.vector.tensor_tensor(s["inn"], s["ss"], s["a"], ALU.subtract))
                ask(nc.vector.tensor_scalar(s["inn"], s["inn"], EPS, None, ALU.max))

            norm_stats(0)
            for c in range(BC):
                if c + 1 < BC:
                    norm_stats(c + 1)
                norm(c)
            for stage in range(3):
                log_map(0, stage)

            dve.wait_ge(s_const, 16 * N_CONST)
            nc.vector.tensor_scalar(omu_sb[:, :, :], mu_sb[:, :, :], -1.0, 1.0, ALU.mult, ALU.add).then_inc(s_omu, 1)

            def to_token(c):
                after(dve, s_tr, c - 1)
                for j in range(CB):
                    blk = c * CB + j
                    last = nc.vector.tensor_scalar(token[:, c % 2, j, :], y_sb[:, blk, :],
                                                   sc["f"][:, blk:blk + 1], None, ALU.mult)
                last.then_inc(s_token, 1)

            def clip(c, t):
                dve.wait_ge(s_proj, c * 4 + t + 1)
                after(dve, s_rest, (c - 1) * 4 + t + 1)
                after(dve, s_square, (c - 1) * 4 + t + 1)
                nc.vector.tensor_scalar(clipped[0:SR, t, :], ps[0:SR, t % 2, :], -5.0, 5.0,
                                        ALU.max, ALU.min).then_inc(s_clipped, 1)

            def later_parts(c, t):
                dve.wait_ge(s_rest, c * 4 + t + 1)
                nc.vector.tensor_copy(parts[0:SR, t, 1, :], rest[0:SR, t, :]).then_inc(s_p1, 1)
                dve.wait_ge(s_p1, c * 4 + t + 1)
                nc.vector.tensor_tensor(parts[0:SR, t, 2, :], rest[0:SR, t, :], parts[0:SR, t, 1, :],
                                        ALU.subtract).then_inc(s_p2, 1)

            def sign(c):
                dve.wait_ge(s_root, c + 1)
                after(dve, s_z2, c - 1)
                nc.vector.tensor_scalar(dim0[:, c % 2, :], root[:, c % 2, :], sign_sb[:, 0:1], None,
                                        ALU.mult).then_inc(s_dim0, 1)

            def later_parts0(c):
                dve.wait_ge(s_zrest, c + 1)
                nc.vector.tensor_copy(parts0[:, c % 2, 1, :], dim0[:, c % 2, :]).then_inc(s_z1, 1)
                dve.wait_ge(s_z1, c + 1)
                nc.vector.tensor_tensor(parts0[:, c % 2, 2, :], dim0[:, c % 2, :], parts0[:, c % 2, 1, :],
                                        ALU.subtract).then_inc(s_z2, 1)

            def sum_groups(g, buf, loaded):
                dve.wait_ge(s_k[buf], loaded)
                for n in range(2):
                    last = nc.vector.tensor_tensor(half_sums[:, n, :], kT[0:ROWS, buf, 2 * n * NG:(2 * n + 1) * NG],
                                                   kT[0:ROWS, buf, (2 * n + 1) * NG:(2 * n + 2) * NG], ALU.add)
                last.then_inc(s_half, 1)
                dve.wait_ge(s_half, g + 1)
                nc.vector.tensor_tensor(group_sums[:, buf, :], half_sums[:, 0, :], half_sums[:, 1, :],
                                        ALU.add).then_inc(s_gsum, 1)

            def max_groups(g, buf, j, bank):
                dve.wait_ge(s_gps, g * KB + (j + 1))
                nc.vector.tensor_reduce(group_max[:, buf, j:j + 1], ps[:, bank, :], AX_X,
                                        ALU.max).then_inc(s_gmax, 1)

            def set_shift(g, buf, bank):
                dve.wait_ge(s_shT, g + 1)
                nc.vector.tensor_scalar(shift_row[:, :], ps[0:KB, bank, 0:P], -1.0 / GROUP, -SHIFT * DH ** 0.5,
                                        ALU.mult, ALU.add).then_inc(s_shrow, 1)
                dve.wait_ge(s_shrow, g + 1)
                nc.vector.tensor_tensor(qT[ROWS:ROWS + KB, buf, :].rearrange("r (j q) -> r j q", j=KB),
                                        shift_row[:, :].unsqueeze(1).broadcast_to([KB, KB, P]),
                                        diag_sb[:, :].unsqueeze(2).broadcast_to([KB, KB, P]),
                                        ALU.mult).then_inc(s_shift, 1)

            def norm_step(c, step):
                n = NORM_STEPS.get((c, step))
                if n and n[1] == "stats":
                    norm_stats(n[0])
                elif n:
                    norm(n[0], n[1])

            def first_maxima(c, step):
                for j in GROUPS_AT.get((c, step), ()):
                    max_groups(0, 0, j, 3)

            to_token(0)
            to_token(1)
            for c in range(CHUNKS):
                if c == BC + 1:
                    sum_groups(0, 0, 16 * LOADS)
                clip(c, 0)
                if c > 0:
                    sign(c - 1)
                first_maxima(c, 0)
                clip(c, 1)
                first_maxima(c, 1)
                if c == BC - 1:
                    log_map(1, 0)
                later_parts(c, 0)
                first_maxima(c, 2)
                norm_step(c, 0)
                clip(c, 2)
                if c == BC - 1:
                    log_map(1, 1)
                first_maxima(c, 3)
                later_parts(c, 1)
                norm_step(c, 1)
                if c + 1 < CHUNKS:
                    first_maxima(c, 4)
                clip(c, 3)
                if c == BC - 1:
                    log_map(1, 2)
                    to_token(c + 1)
                if c + 1 < CHUNKS:
                    first_maxima(c, 5)
                else:
                    set_shift(0, 0, 3)
                if c > 0:
                    later_parts0(c - 1)
                later_parts(c, 2)
                norm_step(c, 2)
                later_parts(c, 3)
                norm_step(c, 3)
                if c != BC - 2 and c + 2 < CHUNKS:
                    to_token(c + 2)
            sign(CHUNKS - 1)
            later_parts0(CHUNKS - 1)

            def exp_map(b):
                s = {n: small(n, b) for n in sc}
                if b == 0:
                    even, odd, m2_even, m2_odd = (statistic(n, b, KB) for n in (1, 4, 2, 5))
                    dve.wait_ge(e_bn0, BC)
                    nc.vector.scalar_tensor_tensor(s["a"], even, float(D // 2), even, ALU.mult, ALU.mult)
                    nc.vector.scalar_tensor_tensor(s["t"], odd, float(D // 2 - 1), odd, ALU.mult, ALU.mult)
                    link(nc.vector.tensor_tensor(s["ss"], m2_even, m2_odd, ALU.add))
                    link(nc.vector.tensor_tensor(s["a"], s["a"], s["t"], ALU.add))
                    ask(nc.vector.tensor_tensor(s["ss"], s["ss"], s["a"], ALU.add))
                wait_answer()
                link(nc.vector.tensor_scalar(s["u"], s["u"], 5.0, None, ALU.min))
                nc.vector.tensor_scalar(s["dn"], s["u"], EPS, None, ALU.add)
                link(nc.vector.tensor_tensor(s["t"], s["u"], s["u"], ALU.mult))
                nc.vector.reciprocal(s["dn"], s["dn"])
                link(nc.vector.tensor_scalar(s["a"], s["t"], 1.0 / factorial(2 * SINH_TERMS + 1), None, ALU.mult))
                for k in range(SINH_TERMS - 1, 0, -1):
                    link(nc.vector.scalar_tensor_tensor(s["a"], s["a"], 1.0 / factorial(2 * k + 1), s["t"],
                                                        ALU.add, ALU.mult))
                link(nc.vector.tensor_tensor(s["dn"], s["dn"], s["u"], ALU.mult))
                link(nc.vector.scalar_tensor_tensor(s["f"], s["a"], 1.0, s["dn"], ALU.add, ALU.mult))
                link(nc.vector.reciprocal(s["d"], s["f"]))
                nc.vector.tensor_scalar(s["hi"], s["d"], 8.0, None, ALU.mult)
                link(nc.vector.tensor_scalar(s["lo"], s["d"], -8.0, None, ALU.mult))

            def clip_rows(first, n):
                for c in range(first, first + n):
                    for j in range(CB):
                        blk = c * CB + j
                        last = nc.vector.tensor_scalar(v_sb[:, blk, :], v_sb[:, blk, :], sc["lo"][:, blk:blk + 1],
                                                       sc["hi"][:, blk:blk + 1], ALU.max, ALU.min)
                    last.then_inc(e_clip, 1)
                    dve.wait_ge(e_clip, c + 1)
                    layer_stats(v_sb, e_bn, c, first=1)

            def copy_out(g, buf):
                dve.wait_ge(s_pv, g * KB + KB)
                nc.vector.tensor_copy(oT[:, buf, :], ps[:, 6 + buf, :]).then_inc(s_oT, 1)

            def divide(g, buf):
                dve.wait_ge(s_otr, g + 1)
                tokens = ps[:, 6 + buf, :].rearrange("p (j c i) -> p j c i", j=CB, c=QC)
                nc.vector.reciprocal(rden[:, buf, :, :], tokens[:, :, :, DH:DH + 1].rearrange("p j c o -> p j (c o)")
                                     ).then_inc(s_rden, 1)
                dve.wait_ge(s_rden, g + 1)
                nc.vector.tensor_tensor(
                    o_heads[:, bass.ds(g, 1), :, :].rearrange("p g k i -> p (g k) i").rearrange(
                        "p (c j) i -> p j c i", j=CB),
                    tokens[:, :, :, 0:DH], rden[:, buf, :, :].unsqueeze(3).broadcast_to([P, CB, QC, DH]),
                    ALU.mult).then_inc(s_out, 1)

            def head(g, buf, first, last, loaded):
                if not first:
                    copy_out(g - 1, 1 - buf)
                    divide(g - 1, 1 - buf)
                if not last:
                    sum_groups(g + 1, 1 - buf, loaded)
                    for j in range(KB):
                        max_groups(g + 1, 1 - buf, j, 4 + j % 2)
                    set_shift(g + 1, 1 - buf, 4)

            head(0, 0, True, False, 16 * LOADS)
            with dve.Fori(0, HEADS // 2 - 1) as i:
                head(i * 2 + 1, 1, False, False, i * (16 * LOADS) + 2 * 16 * LOADS)
                head(i * 2 + 2, 0, False, False, i * (16 * LOADS) + 2 * 16 * LOADS)
            head(HEADS - 1, 1, False, True, 0)
            for c in range(BC):
                dve.wait_ge(e_tr, c + 1)
                after(dve, e_wo, 2 * (c - 1))
                nc.vector.tensor_copy(vT[:, c % 2, :, :], ps[:, 4:6, :]).then_inc(e_trc, 1)
                dve.wait_ge(e_wo, c * 2 + 2)
                nc.vector.tensor_copy(blocks(v_sb, c * CB, CB), ps[:, 4:6, :].rearrange("p a b -> p (a b)")
                                      ).then_inc(e_woc, 2)
                dve.wait_ge(e_woc, c * 2 + 2)
                layer_stats(v_sb, e_bn0, c, first=1)
            exp_map(0)
            clip_rows(0, BC)
            copy_out(HEADS - 1, 1)
            divide(HEADS - 1, 1)

            def out_norm(b):
                s = {n: small(n, b) for n in sc}
                even, odd, m2_even, m2_odd = (statistic(n, b, KB) for n in (1, 4, 2, 5))
                ne, no = D // 2, D // 2 - 1
                dve.wait_ge(e_bn, (b + 1) * BC)
                nc.vector.tensor_scalar(s["z"], even, float(ne) / (D - 1), None, ALU.mult)
                nc.vector.tensor_tensor(s["m2"], m2_even, m2_odd, ALU.add)
                link(nc.vector.tensor_tensor(s["a"], even, odd, ALU.subtract))
                nc.vector.scalar_tensor_tensor(s["z"], odd, float(no) / (D - 1), s["z"], ALU.mult, ALU.add)
                link(nc.vector.scalar_tensor_tensor(s["a"], s["a"], float(ne * no) / (D - 1), s["a"], ALU.mult, ALU.mult))
                nc.vector.tensor_tensor(s["z"], s["z"], s["f"], ALU.mult)
                nc.vector.tensor_tensor(s["t"], s["f"], s["f"], ALU.mult)
                link(nc.vector.tensor_tensor(s["m2"], s["m2"], s["a"], ALU.add))
                link(nc.vector.tensor_tensor(s["m2"], s["m2"], s["t"], ALU.mult))
                link(nc.vector.scalar_tensor_tensor(s["a"], s["z"], float(D - 1), s["z"], ALU.mult, ALU.mult))
                ask(nc.vector.tensor_tensor(s["inn"], s["m2"], s["a"], ALU.add))
                wait_answer()
                nc.vector.tensor_tensor(s["w"], s["y0"], s["z"], ALU.subtract)
                link(nc.vector.tensor_tensor(v_sb[:, b * KB:(b + 1) * KB, 0:1].rearrange("p n o -> p (n o)"),
                                             s["y0"], s["d"], ALU.mult))
                link(nc.vector.scalar_tensor_tensor(s["a"], s["w"], float(D - 1) / D, s["w"], ALU.mult, ALU.mult))
                link(nc.vector.tensor_tensor(s["var"], s["m2"], s["a"], ALU.add))
                ask(nc.vector.tensor_scalar(s["var"], s["var"], 1.0 / D, None, ALU.mult))
                link(nc.vector.scalar_tensor_tensor(s["mean"], s["w"], 1.0 / D, s["z"], ALU.mult, ALU.add))
                link(nc.vector.tensor_tensor(s["shift"], s["mean"], s["d"], ALU.mult))
                wait_answer()
                link(nc.vector.reciprocal(s["rstd"], s["sd"]))
                link(nc.vector.tensor_tensor(s["scale"], s["rstd"], s["f"], ALU.mult))

            def normalise(dst, src, c, shift="mean", scale="rstd"):
                for j in range(CB):
                    blk = c * CB + j
                    last = nc.vector.tensor_scalar(dst(j), src[:, blk, :], sc[shift][:, blk:blk + 1],
                                                   sc[scale][:, blk:blk + 1], ALU.subtract, ALU.mult)
                return last

            def residual(b):
                for c in range(b * BC, (b + 1) * BC):
                    normalise(lambda j, c=c: v_sb[:, c * CB + j, :], v_sb, c, "shift", "scale").then_inc(e_norm, 1)
                for c in range(b * BC, (b + 1) * BC):
                    dve.wait_ge(e_x1, c + 1)
                    layer_stats(x_sb, e_bn1, c)

            def ask_sd(b, done, count, n=KB):
                dve.wait_ge(done, count)
                ask(combine_stats(b, n))

            def take_rstd(b, n=KB):
                wait_answer()
                link(nc.vector.reciprocal(small("rstd", b, n), small("sd", b, n)))

            def to_tokens(c):
                after(dve, f_tr, c - 1)
                normalise(lambda j: token[:, c % 2, j, :], x_sb, c).then_inc(f_token, 1)

            def mix(c):
                after(dve, f_r, c - 1)
                for w in (1, 0):
                    dve.wait_ge(f_prev, c * 2 + 2)
                    for k in range(KT):
                        last = nc.vector.scalar_tensor_tensor(mixed[:, c % 2, w, k, :], xT[:, c % 2, k, 1:CT + 1],
                                                              mu_sb[:, w, k:k + 1], mix_prev[:, c % 2, w, k, :],
                                                              ALU.mult, ALU.add)
                    last.then_inc(f_mix, 1)

            def gated(c):
                dve.wait_ge(f_kv, c * 2 + 2)
                dve.wait_ge(f_sig, c + 1)
                nc.vector.tensor_tensor(blocks(y_sb, c * CB, CB), vT[:, c % 2, :, :].rearrange("p a b -> p (a b)"),
                                        ps[:, 6:8, :].rearrange("p a b -> p (a b)"), ALU.mult).then_inc(f_o, 1)
                dve.wait_ge(f_o, c + 1)
                layer_stats(y_sb, f_bn, c)

            def finish(c):
                normalise(lambda j: y_sb[:, c * CB + j, :], y_sb, c).then_inc(f_norm, 1)
                if c < BC:
                    return
                dve.wait_ge(f_norm, c + 1)
                nc.vector.tensor_tensor(blocks(y_sb, c * CB, CB), blocks(y_sb, c * CB, CB),
                                        blocks(x_sb, c * CB, CB), ALU.add).then_inc(f_out[1], 1)

            out_norm(0)
            residual(0)
            ask_sd(0, e_bn1, BC)
            take_rstd(0)
            to_tokens(0)
            to_tokens(1)
            mix(0)
            exp_map(1)
            to_tokens(2)
            mix(1)
            clip_rows(BC, 2)
            mix(2)
            gated(0)
            to_tokens(3)
            clip_rows(BC + 2, 2)
            out_norm(1)
            mix(3)
            gated(1)
            residual(1)
            ask_sd(1, e_bn1, 2 * BC)
            take_rstd(1)
            to_tokens(4)
            for c in range(2, CHUNKS):
                if c + 2 < CHUNKS:
                    mix(c + 2)
                if c == BC + 1:
                    take_rstd(0)
                if c == BC + 3:
                    finish(BC + 1)
                gated(c)
                if c + 3 < CHUNKS:
                    to_tokens(c + 3)
                if c == BC:
                    ask_sd(0, f_bn, BC)
                if c == BC + 1:
                    ask_sd(2, f_bn, BC + 2, 2 * CB)
                    finish(0)
                    finish(1)
                if c == BC + 2:
                    take_rstd(2, 2 * CB)
                    ask_sd(c, f_bn, c + 1, CB)
                    finish(2)
                    finish(3)
                    finish(BC)
            ask_sd(CHUNKS - 1, f_bn, CHUNKS, CB)
            take_rstd(CHUNKS - 2, CB)
            finish(CHUNKS - 2)
            take_rstd(CHUNKS - 1, CB)
            finish(CHUNKS - 1)

        @block.tensor
        def _(pe):
            pe.wait_ge(s_const, 16 * N_CONST)

            def transposes(par, done):
                for k in range(KT):
                    for j in range(CB):
                        last = nc.tensor.transpose(ps[:, 4 + k, j * P:(j + 1) * P],
                                                   token[:, par, j, k * P:(k + 1) * P], ident_sb[:, :])
                last.then_inc(done, 1)

            def by_token(bank, j, left, w):
                for k in range(KT):
                    last = nc.tensor.matmul(ps[:, bank, (j % 2) * D:(j % 2 + 1) * D], left[:, k, j * P:(j + 1) * P],
                                            w[:, k, :], start=(k == 0), stop=(k == KT - 1))
                return last

            def by_dim(bank, dt, w, right, rows=P):
                for k in range(KT):
                    last = nc.tensor.matmul(ps[0:rows, bank, :], w[:, k, dt * rows:(dt + 1) * rows], right[:, k, :],
                                            start=(k == 0), stop=(k == KT - 1))
                return last

            def turn(c):
                pe.wait_ge(s_token, c + 1)
                after(pe, s_vT, c)
                transposes(c % 2, s_tr)

            def project(c, t):
                after(pe, s_clipped, c * 4 + t - 1)
                by_dim(t % 2, t % 2, w_sb["q" if t < 2 else "k"], vT[:, c % 2], SR).then_inc(s_proj, 1)

            def norms(c):
                pe.wait_ge(s_square, c * 4 + 4)
                after(pe, s_root, c)
                for dt in range(2):
                    for n in range(2):
                        last = nc.tensor.matmul(ps[n * VW:(n + 1) * VW, 2, :], headsum_sb[:, dt, :],
                                                square[0:SR, 2 * n + dt, :], start=(dt == 0), stop=(dt == 1))
                last.then_inc(s_norms, 1)

            def values(c, n):
                after(pe, s_vcopy, (c - 1) * 2 + n + 1)
                for j in range(2):
                    last = by_token(6 + n, 2 * n + j, vT[:, c % 2], w_sb["v"])
                last.then_inc(s_vps, 1)

            def group_scores(g, buf, j, bank):
                if j == 0:
                    pe.wait_ge(s_gsum, g + 1)
                    after(pe, s_shrow, g)
                after(pe, s_gmax, g * KB + (j if bank == 3 else j - 1))
                nc.tensor.matmul(ps[:, bank, :], qT[0:ROWS, buf, j * P:(j + 1) * P], group_sums[:, buf, :],
                                 start=True, stop=True).then_inc(s_gps, 1)

            def turn_max(g, buf, bank):
                pe.wait_ge(s_gmax, g * KB + KB)
                nc.tensor.transpose(ps[0:KB, bank, 0:P], group_max[:, buf, :], ident_sb[:, :]).then_inc(s_shT, 1)

            def first_groups(c, step):
                for j in GROUPS_AT.get((c, step), ()):
                    group_scores(0, 0, j, 3)

            turn(0)
            for c in range(CHUNKS):
                if c > 0:
                    norms(c - 1)
                pe.wait_ge(s_vT, c + 1)
                project(c, 0)
                if c == BC + 1:
                    pe.wait_ge(s_q[0], 16 * LOADS)
                first_groups(c, 0)
                project(c, 1)
                first_groups(c, 1)
                values(c, 0)
                first_groups(c, 2)
                project(c, 2)
                first_groups(c, 3)
                if c + 1 < CHUNKS:
                    values(c, 1)
                    first_groups(c, 4)
                    project(c, 3)
                    first_groups(c, 5)
                    turn(c + 1)
                else:
                    project(c, 3)
                    turn_max(0, 0, 3)
                    values(c, 1)
            norms(CHUNKS - 1)

            def scores(g, buf, kb, half):
                if kb == 0 and half == 0:
                    pe.wait_ge(s_shift, g + 1)
                after(pe, s_exp, g * (2 * KB) + (kb * 2 + half - 1))
                for n in range(2):
                    q0 = (half * 2 + n) * CT
                    last = nc.tensor.matmul(ps[:, half * 2 + n, :], kT[0:ROWS + KB, buf, kb * P:(kb + 1) * P],
                                            qT[0:ROWS + KB, buf, q0:q0 + CT], start=True, stop=True)
                last.then_inc(s_scores, 1)

            def weigh(g, buf, kb):
                pe.wait_ge(s_exp, g * (2 * KB) + (kb * 2 + 2))
                if kb == 0:
                    pe.wait_ge(s_vhead, g + 1)
                    after(pe, s_out, g - 1)
                for c in range(QC):
                    last = nc.tensor.matmul(ps[c * VW:(c + 1) * VW, 6 + buf, :], v_head[:, buf, kb, :],
                                            probs[:, kb % 4, c * CT:(c + 1) * CT], start=(kb == 0), stop=(kb == KB - 1))
                last.then_inc(s_pv, 1)

            def turn_out(g, buf):
                pe.wait_ge(s_oT, g + 1)
                for j in range(CB):
                    last = nc.tensor.transpose(ps[:, 6 + buf, j * P:(j + 1) * P], oT[:, buf, j * P:(j + 1) * P], ident_sb[:, :])
                last.then_inc(s_otr, 1)

            def turn_attention(c):
                pe.wait_ge(e_token, c + 1)
                after(pe, e_trc, c)
                after(pe, e_woc, 2 * min(c, BC))
                transposes(c % 2, e_tr)

            def out_product(c, bank):
                pe.wait_ge(e_trc, c + 1)
                for n in range(2):
                    after(pe, e_woc, (c - 1) * 2 + n + 1)
                    for j in range(2):
                        last = by_token(bank + n, 2 * n + j, vT[:, c % 2], w_sb["o"])
                    last.then_inc(e_wo, 1)

            def head(g, buf, first, last, loaded):
                for kb in range(KB):
                    scores(g, buf, kb, 1)
                    if kb > 0:
                        weigh(g, buf, kb - 1)
                    elif not first:
                        weigh(g - 1, 1 - buf, KB - 1)
                    if kb + 1 < KB:
                        scores(g, buf, kb + 1, 0)
                    elif not last:
                        scores(g + 1, 1 - buf, 0, 0)
                    if kb == 1 and not first:
                        turn_out(g - 1, 1 - buf)
                    if kb == G_FIRST and not last:
                        pe.wait_ge(s_q[1 - buf], loaded)
                    if G_FIRST <= kb < G_FIRST + G_STEPS and not last:
                        for j in range((kb - G_FIRST) * KB // G_STEPS, (kb - G_FIRST + 1) * KB // G_STEPS):
                            group_scores(g + 1, 1 - buf, j, 4 + j % 2)
                    if kb == G_FIRST + G_STEPS and not last:
                        turn_max(g + 1, 1 - buf, 4)
                    if last and kb < 2 * BC:
                        if kb % 2 == 0:
                            turn_attention(kb // 2)
                        else:
                            out_product(kb // 2, 4)

            pe.wait_ge(s_memset, 8)
            pe.wait_ge(s_clipped, 4 * CHUNKS)
            pe.wait_ge(s_root, CHUNKS)
            pe.wait_ge(s_vcopy, 2 * CHUNKS)
            scores(0, 0, 0, 0)
            head(0, 0, True, False, 16 * LOADS)
            with pe.Fori(0, HEADS // 2 - 1) as i:
                head(i * 2 + 1, 1, False, False, i * (16 * LOADS) + 2 * 16 * LOADS)
                head(i * 2 + 2, 0, False, False, i * (16 * LOADS) + 2 * 16 * LOADS)
            head(HEADS - 1, 1, False, True, 0)
            weigh(HEADS - 1, 1, KB - 1)
            turn_out(HEADS - 1, 1)

            pe.wait_ge(s_out, HEADS)
            turn_attention(BC)
            for c in range(BC, CHUNKS):
                pe.wait_ge(e_trc, c + 1)
                if c + 1 < CHUNKS:
                    turn_attention(c + 1)
                out_product(c, 6)

            def turn_tokens(c):
                pe.wait_ge(f_token, c + 1)
                after(pe, f_xT, 2 * c)
                transposes(c % 2, f_tr)

            pe.wait_ge(e_woc, 2 * CHUNKS)
            turn_tokens(0)
            turn_tokens(1)

            def product_k(c):
                pe.wait_ge(f_mix, 2 * c + 1)
                for dt in range(KT):
                    after(pe, f_relu, (c - 1) * KT + dt + 1)
                    by_dim(2 + dt, dt, w_sb["kf"], mixed[:, c % 2, 1]).then_inc(f_k, 1)

            def product_r(c):
                pe.wait_ge(f_mix, 2 * c + 2)
                after(pe, f_sig, c)
                for j in range(CB):
                    last = by_token(j // 2, j, mixed[:, c % 2, 0], w_sb["r"])
                last.then_inc(f_r, 1)

            def product_kv(c):
                pe.wait_ge(f_sq, c * KT + KT)
                after(pe, f_o, c)
                for n in range(2):
                    for j in range(2):
                        last = by_token(6 + n, 2 * n + j, square[:, 2:4], w_sb["vf"])
                    last.then_inc(f_kv, 1)

            product_k(0)
            product_r(0)
            for c in range(CHUNKS):
                if c + 2 < CHUNKS:
                    turn_tokens(c + 2)
                if c + 1 < CHUNKS:
                    product_k(c + 1)
                product_kv(c)
                if c + 1 < CHUNKS:
                    product_r(c + 1)


def kernel(L0_attn_x, L0_attn_Wq, L0_attn_Wk, L0_attn_Wv, L0_attn_Wo, L0_ffn_W_r, L0_ffn_W_k, L0_ffn_W_v,
           L0_ffn_mu_r, L0_ffn_mu_k):
    import numpy as np
    import concourse.bacc as bacc
    from concourse.bass_utils import run_bass_kernel_spmd

    ident = np.eye(P, dtype=np.float32)
    row = np.arange(2 * SR).reshape(2, SR).T
    headsum = (row[:, :, None] % H == np.arange(VW)).astype(np.float32)
    sign = np.where(np.arange(2 * VW) < VW, -1.0, 1.0).astype(np.float32)[:, None]

    def dim_major(w):
        return np.ascontiguousarray(np.asarray(w).reshape(H, DH, D)[:, 1:].transpose(2, 1, 0).reshape(D, 2 * SR))

    arrays = {
        "x": np.ascontiguousarray(L0_attn_x).reshape(B * T, D),
        "wq": dim_major(L0_attn_Wq),
        "wk": dim_major(L0_attn_Wk),
        "wv": np.ascontiguousarray(np.asarray(L0_attn_Wv).T),
        "wo": np.ascontiguousarray(np.asarray(L0_attn_Wo).T),
        "wr": np.ascontiguousarray(np.asarray(L0_ffn_W_r).T),
        "wkf": np.ascontiguousarray(np.asarray(L0_ffn_W_k).T),
        "wvf": np.ascontiguousarray(np.asarray(L0_ffn_W_v).T),
        "mus": np.ascontiguousarray(np.stack([np.asarray(m).reshape(KT, P).T for m in (L0_ffn_mu_r, L0_ffn_mu_k)], 1)),
        "ident": ident, "headsum": headsum, "sign": sign, "diag": np.eye(KB, dtype=np.float32),
    }
    nc = bacc.Bacc("TRN2", target_bir_lowering=False, num_devices=1)
    args = [nc.dram_tensor(f"in_{n}", a.shape, mybir.dt.from_np(a.dtype), kind="ExternalInput").ap()
            for n, a in arrays.items()]
    args.append(nc.dram_tensor("out_0", (B * T, D), F32, kind="ExternalOutput").ap())
    sandwich(nc, *args)
    r = run_bass_kernel_spmd(nc, [{f"in_{n}": a for n, a in arrays.items()}], core_ids=[0])
    return r.results[0]["out_0"].reshape(B, T, D)
```

```python
from contextlib import ExitStack
from math import factorial

import concourse.bass as bass
from concourse import mybir

P = 128
F32 = mybir.dt.float32
BF16 = mybir.dt.bfloat16
ACT = mybir.ActivationFunctionType
ALU = mybir.AluOpType
AX_X = mybir.AxisListType.X

B, T, D, H = 2, 2048, 256, 16
DH = D // H
HEADS = B * H
BLOCKS = B * T // P
KB = T // P
CB = 4
BC = KB // CB
CHUNKS = B * BC
CT = CB * P
KT = D // P
PARTS = 3
PAIRS = ((0, 0), (0, 1), (0, 2), (1, 0), (1, 1), (2, 0))
ROWS = len(PAIRS) * DH
GROUP = 4
NG = T // GROUP
VW = 32
QC = T // CT
EPS = 1e-6
LN_EPS = 1e-5
SHIFT = 65.0
SINH_TERMS = 14
SR = (DH - 1) * H // 2
LOADS = PARTS
G_FIRST, G_STEPS = 0, 13
X1_POOL = 2
OUT_POOL = 7
OUT_ROOT = 10
NORM_STEPS = {(n // 4, n % 4): (BC + c, part) for n, (c, part) in enumerate((
    (0, "stats"), (1, "stats"), (0, 0), (0, 1), (2, "stats"), (1, 0), (1, 1), (3, "stats"), (2, 0), (2, 1),
    (3, 0), (3, 1)))}
GROUPS_AT = {}
for query_block in range(KB):
    step = 2 + query_block - (query_block > 7) - (query_block > 9)
    GROUPS_AT.setdefault((BC + 1 + step // 6, step % 6), []).append(query_block)


def sandwich(nc, x, wq, wk, wv, wo, wr, wkf, wvf, mus, ident, headsum, sign, diag, out):
    with ExitStack() as ctx:
        def sb(name, shape, dt=F32):
            return ctx.enter_context(nc.sbuf_tensor(name, shape, dt))

        def sem(name):
            return ctx.enter_context(nc.semaphore(name))

        q_parts = nc.dram_tensor("q_parts", (PARTS, B, DH, H, T), BF16, kind="Internal").ap()
        k_parts = nc.dram_tensor("k_parts", (PARTS, B, DH, H, T), BF16, kind="Internal").ap()

        w_sb = {n: sb(f"w_{n}", [P, KT, 2 * SR if n in "qk" else D]) for n in ("q", "k", "v", "o", "r", "kf", "vf")}
        ident_sb = sb("ident_sb", [P, P])
        headsum_sb = sb("headsum_sb", [SR, 2, VW])
        sign_sb = sb("sign_sb", [2 * VW, 1])
        diag_sb = sb("diag_sb", [KB, KB])
        mu_sb = sb("mu_sb", [P, 2, KT])
        omu_sb = sb("omu_sb", [P, 2, KT])
        one_eps = sb("one_eps", [P, 1])
        ln_eps = sb("ln_eps", [P, 1])
        eps_col = sb("eps_col", [P, 1])
        one_col = sb("one_col", [P, 1])
        zero_col = sb("zero_col", [P, KT])

        x_sb = sb("x_sb", [P, BLOCKS, D])
        y_sb = sb("y_sb", [P, BLOCKS, D])
        v_sb = sb("v_sb", [P, BLOCKS, D])
        by_head = "p (g k i) -> p g k i"
        v_heads = v_sb[:, :, :].rearrange("p a b -> p (a b)").rearrange(by_head, g=HEADS, k=KB)
        o_heads = y_sb[:, :, :].rearrange("p a b -> p (a b)").rearrange(by_head, g=HEADS, k=KB)

        work = sb("work", [P, 4 * T])
        clipped, rest = (work[:, n * T:(n + 1) * T].rearrange("p (t n) -> p t n", t=4) for n in range(2))
        root, dim0 = (work[0:2 * VW, (4 + n) * T // 2:(5 + n) * T // 2].rearrange("p (b n) -> p b n", b=2)
                      for n in range(2))
        parts0 = work[0:2 * VW, 3 * T:3 * T + PARTS * CT].bitcast(BF16).rearrange("p (b s n) -> p b s n", b=2, s=PARTS)
        probs = work[:, :].rearrange("p (n q) -> p n q", n=4)
        xT = work[:, 0:2 * KT * (CT + 1)].rearrange("p (b k t) -> p b k t", b=2, k=KT)
        mixed = work[:, T + 16:3 * T + 16].rearrange("p (b w k t) -> p b w k t", b=2, w=2, k=KT)
        mix_prev = v_sb[:, :, :].rearrange("p a b -> p (a b)")[:, 0:4 * KT * CT].rearrange(
            "p (b w k t) -> p b w k t", b=2, w=2, k=KT)
        token = sb("token", [P, 2, CB, D])
        vT = sb("vT", [P, 2, KT, CT])
        square = sb("square", [P, 4, CT])
        unread = sb("unread", [P, 2, D])
        parts = sb("parts", [P, 4, PARTS, CT], BF16)

        spare = parts[:, :, :, :].rearrange("p t s n -> p (t s n)")
        q_two, k_two = sb("q_two", [P, 2, T], BF16), sb("k_two", [P, 2, T], BF16)
        qT = [q_two[:, 0, :], q_two[:, 1, :], spare[:, 0:T]]
        kT = [k_two[:, 0, :], k_two[:, 1, :], spare[:, T:2 * T]]
        half_sums = unread[0:ROWS, :, :].rearrange("p a b -> p (a b)").bitcast(BF16).rearrange("p (n k) -> p n k", n=2)
        group_sums = sb("group_sums", [ROWS, 2, NG], BF16)
        v_head = sb("v_head", [P, 2, KB, VW])
        group_max = sb("group_max", [P, 2, KB])
        shift_row = sb("shift_row", [KB, P])
        oT = square[:, 0:2, :]
        rden = sb("rden", [P, 2, CB, QC])

        stats = sb("stats", [P, BLOCKS, 6])
        sc = {n: sb(f"sc_{n}", [P, BLOCKS]) for n in
              ("sd", "rstd", "ss", "y0", "z", "t", "u", "w", "d", "d0", "inn", "f", "a", "dn", "mean", "var", "m2", "lo",
               "hi", "shift", "scale")}

        ps = ctx.enter_context(nc.psum_tensor("ps", [P, 8, CT], F32))

        s_const = sem("s_const")
        s_memset = sem("s_memset")
        s_omu = sem("s_omu")
        s_x = [sem(f"s_x{c}") for c in range(CHUNKS)]
        s_bn, s_var, s_sd, s_norm, s_clip, s_ss = map(sem, ("s_bn", "s_var", "s_sd", "s_norm", "s_clip", "s_ss"))
        s_link = sem("s_link")
        s_ask = sem("s_ask")
        s_answer = sem("s_answer")
        s_token, s_tr, s_vT = map(sem, ("s_token", "s_tr", "s_vT"))
        s_vps, s_vcopy = map(sem, ("s_vps", "s_vcopy"))
        s_proj, s_clipped, s_square, s_p0, s_rest, s_p1, s_p2 = map(
            sem, ("s_proj", "s_clipped", "s_square", "s_p0", "s_rest", "s_p1", "s_p2"))
        s_norms, s_root, s_dim0, s_z0, s_zrest, s_z1, s_z2 = map(
            sem, ("s_norms", "s_root", "s_dim0", "s_z0", "s_zrest", "s_z1", "s_z2"))
        s_store = [sem(f"s_store{n}") for n in range(4)]
        s_store0 = [sem(f"s_store0_{n}") for n in range(2)]
        s_q = [sem(f"s_q{n}") for n in range(3)]
        s_k = [sem(f"s_k{n}") for n in range(3)]
        s_half, s_gsum, s_vhead, s_gps, s_gmax, s_shT, s_shrow, s_shift = map(
            sem, ("s_half", "s_gsum", "s_vhead", "s_gps", "s_gmax", "s_shT", "s_shrow", "s_shift"))
        s_scores, s_exp, s_pv, s_oT, s_otr, s_rden, s_out = map(
            sem, ("s_scores", "s_exp", "s_pv", "s_oT", "s_otr", "s_rden", "s_out"))
        e_token, e_tr, e_trc, e_wo, e_woc, e_ss = map(sem, ("e_token", "e_tr", "e_trc", "e_wo", "e_woc", "e_ss"))
        e_bn0, e_clip, e_bn, e_norm, e_x1, e_bn1 = map(sem, ("e_bn0", "e_clip", "e_bn", "e_norm", "e_x1", "e_bn1"))
        f_token, f_tr, f_xT, f_prev, f_mix, f_k, f_relu, f_sq = map(
            sem, ("f_token", "f_tr", "f_xT", "f_prev", "f_mix", "f_k", "f_relu", "f_sq"))
        f_r, f_sig, f_kv, f_o, f_bn, f_norm = map(sem, ("f_r", "f_sig", "f_kv", "f_o", "f_bn", "f_norm"))
        f_out_pool, f_out = map(sem, ("f_out_pool", "f_out"))
        s_done = sem("s_done")

        N_CONST = 5 + len(w_sb)
        x_blocks = x.rearrange("(n p) d -> p n d", p=P)
        out_blocks = out.rearrange("(n p) d -> p n d", p=P)

        def blocks(t, first, n=1):
            return t[:, bass.ds(first, n), :].rearrange("p n d -> p (n d)")

        def after(eng, semaphore, value):
            if not isinstance(value, int) or value > 0:
                eng.wait_ge(semaphore, value)

        def loads_of(g):
            return 16 * LOADS * (g // 3 + 1)

        block = ctx.enter_context(nc.Block())

        @block.sync
        def _(sp):
            for c in range(CHUNKS):
                sp.dma_start(x_sb[:, c * CB:(c + 1) * CB, :], x_blocks[:, c * CB:(c + 1) * CB, :]).then_inc(s_x[c], 16)
            for t, a in ((ident_sb[:, :], ident), (headsum_sb[:, :, :], headsum), (sign_sb[:, :], sign),
                         (diag_sb[:, :], diag)):
                sp.dma_start(t, a).then_inc(s_const, 16)
            sp.dma_start(mu_sb[:, :, :], mus).then_inc(s_const, 16)
            for n, a in (("q", wq), ("k", wk), ("v", wv), ("o", wo), ("r", wr), ("kf", wkf), ("vf", wvf)):
                sp.dma_start(w_sb[n][:, :, :], a.rearrange("(k p) d -> p k d", p=P)).then_inc(s_const, 16)

            def store0(c):
                b, cc = c // BC, c % BC
                sp.wait_ge(s_z0, c + 1)
                sp.wait_ge(s_z1, c + 1)
                sp.wait_ge(s_z2, c + 1)
                for n, dst in enumerate((q_parts, k_parts)):
                    sp.dma_start(dst[:, b, 0, :, cc * CT:(cc + 1) * CT].rearrange("s h t -> h s t"),
                                 parts0[n * VW:n * VW + H, c % 2, :, :]).then_inc(s_store0[c % 2], 16)

            def load_head(b, h, buf):
                runs = [(p, PARTS - p, PAIRS.index((p, 0)) * DH) for p in range(PARTS)]
                for p, n, row in runs:
                    sp.dma_start(kT[buf][row:row + n * DH, :],
                                 k_parts[0:n, b, :, bass.ds(h, 1), :].rearrange("s i h t -> s i (h t)")
                                 ).then_inc(s_k[buf], 16)
                for p, n, row in runs:
                    sp.dma_start(qT[buf][row:row + n * DH, :],
                                 q_parts[p:p + 1, b, :, bass.ds(h, 1), :].rearrange("s i h t -> s i (h t)")
                                 .broadcast_to([n, DH, T])).then_inc(s_q[buf], 16)

            def batch_stored(b):
                for t in range(4):
                    sp.wait_ge(s_store[t], 16 * (BC * (b + 1) + (b == 0 and t < 2)))
                for n in range(2):
                    sp.wait_ge(s_store0[n], 32 * BC // 2 * (b + 1))

            for c in range(CHUNKS):
                b, cc = c // BC, c % BC
                for t in range(4):
                    rows = (q_parts, k_parts)[t // 2][:, b, :, :, :].rearrange("s i h t -> (i h) s t")
                    sp.wait_ge(s_p0, c * 4 + t + 1)
                    sp.wait_ge(s_p1, c * 4 + t + 1)
                    sp.wait_ge(s_p2, c * 4 + t + 1)
                    sp.dma_start(rows[H + (t % 2) * SR:H + (t % 2 + 1) * SR, :, cc * CT:(cc + 1) * CT],
                                 parts[0:SR, t, :, :]).then_inc(s_store[t], 16)
                    if t == 1 and c > 0:
                        store0(c - 1)
                    if t == 1 and c == BC:
                        batch_stored(0)
                        load_head(0, 0, 0)
                        load_head(0, 1, 1)
            store0(CHUNKS - 1)
            batch_stored(1)

            def refill(g, b, buf):
                after(sp, s_scores, g * (2 * KB) - 4 * KB)
                load_head(b, g - b * H, buf)

            refill(2, 0, 2)
            with sp.Fori(1, H // 3) as i:
                for n in range(3):
                    refill(i * 3 + n, 0, n)
            for g in (H - 1, H, H + 1):
                refill(g, g // H, g % 3)
            with sp.Fori(H // 3 + 1, HEADS // 3) as i:
                for n in range(3):
                    refill(i * 3 + n, 1, n)
            for g in (HEADS - 2, HEADS - 1):
                refill(g, 1, g % 3)
            for c in range(CHUNKS):
                if c < OUT_POOL:
                    sp.wait_ge(f_out_pool, c + 1)
                else:
                    sp.wait_ge(f_out, c - OUT_POOL + 1)
                sp.dma_start(out_blocks[:, c * CB:(c + 1) * CB, :],
                             y_sb[:, c * CB:(c + 1) * CB, :]).then_inc(s_done, 16)
            sp.wait_ge(s_done, 16 * CHUNKS)

        @block.gpsimd
        def _(pool):
            nc.gpsimd.memset(one_eps[:, :], 1.0 + EPS).then_inc(s_memset, 1)
            nc.gpsimd.memset(ln_eps[:, :], LN_EPS).then_inc(s_memset, 1)
            nc.gpsimd.memset(eps_col[:, :], EPS).then_inc(s_memset, 1)
            nc.gpsimd.memset(one_col[:, :], 1.0).then_inc(s_memset, 1)
            nc.gpsimd.memset(zero_col[:, :], 0.0).then_inc(s_memset, 1)
            nc.gpsimd.memset(v_head[:, :, :, DH + 1:VW], 0.0).then_inc(s_memset, 1)
            nc.gpsimd.memset(v_head[:, :, :, DH:DH + 1], 1.0).then_inc(s_memset, 1)

            pool.wait_ge(s_memset, 7)
            nc.gpsimd.memset(k_two[ROWS:ROWS + KB, :, :], 1.0).then_inc(s_memset, 1)
            pool.wait_ge(s_memset, 8)

            def second_rest(c):
                pool.wait_ge(s_z0, c + 1)
                nc.gpsimd.tensor_tensor(dim0[:, c % 2, :], dim0[:, c % 2, :], parts0[:, c % 2, 0, :],
                                        ALU.subtract).then_inc(s_zrest, 1)

            def load_v(g, buf):
                v = v_heads[:, bass.ds(g, 1), :, :].rearrange("p g k i -> p (g k) i")
                ones = one_col[:, :].unsqueeze(2).broadcast_to([P, KB, DH])
                nc.gpsimd.tensor_tensor(v_head[:, buf, :, 0:DH], v, ones, ALU.mult).then_inc(s_vhead, 1)

            for c in range(CHUNKS):
                for t in range(4):
                    pool.wait_ge(s_p0, c * 4 + t + 1)
                    after(pool, s_p2, (c - 1) * 4 + t + 1)
                    nc.gpsimd.tensor_tensor(rest[0:SR, t, :], clipped[0:SR, t, :], parts[0:SR, t, 0, :],
                                            ALU.subtract).then_inc(s_rest, 1)
                    if t == 1 and c > 0:
                        second_rest(c - 1)
                if c == BC:
                    pool.wait_ge(s_vcopy, 2 * BC)
                    load_v(0, 0)
                    load_v(1, 1)
            second_rest(CHUNKS - 1)

            for t in range(4):
                pool.wait_ge(s_store[t], 16 * CHUNKS)
            nc.gpsimd.memset(kT[2][ROWS:ROWS + KB, :], 1.0).then_inc(s_memset, 1)
            pool.wait_ge(s_vcopy, 2 * CHUNKS)
            with pool.Fori(1, HEADS // 2) as i:
                for buf in range(2):
                    pool.wait_ge(s_pv, i * (2 * KB) + (buf - 1) * KB)
                    load_v(i * 2 + buf, buf)

            def gather(c, first=0, heads=H):
                b, cc = c // BC, c % BC
                for j in range(CB):
                    last = nc.gpsimd.tensor_tensor(
                        token[:, c % 2, j, first * DH:(first + heads) * DH].rearrange("p (h i) -> p h i", h=heads),
                        o_heads[:, b * H + first:b * H + first + heads, cc * CB + j, :],
                        one_col[:, :].unsqueeze(2).broadcast_to([P, heads, DH]), ALU.mult)
                return last

            pool.wait_ge(s_out, H)
            for c in range(BC):
                after(pool, e_tr, c - 1)
                gather(c).then_inc(e_token, 1)
            pool.wait_ge(s_out, HEADS - 1)
            for c in range(BC, BC + 2):
                pool.wait_ge(e_tr, c - 1)
                gather(c, 0, H - 1)
            pool.wait_ge(s_out, HEADS)
            for c in range(BC, BC + 2):
                gather(c, H - 1, 1).then_inc(e_token, 1)
            for c in range(BC + 2, CHUNKS):
                pool.wait_ge(e_tr, c - 1)
                gather(c).then_inc(e_token, 1)

            def residual(c):
                pool.wait_ge(e_norm, c + 1)
                nc.gpsimd.tensor_tensor(blocks(x_sb, c * CB, CB), blocks(x_sb, c * CB, CB),
                                        blocks(v_sb, c * CB, CB), ALU.add).then_inc(e_x1, 1)

            for b in range(B):
                for c in range(b * BC, b * BC + X1_POOL):
                    residual(c)

            for c in range(OUT_POOL):
                pool.wait_ge(f_norm, c + 1)
                nc.gpsimd.tensor_tensor(blocks(y_sb, c * CB, CB), blocks(y_sb, c * CB, CB),
                                        blocks(x_sb, c * CB, CB), ALU.add).then_inc(f_out_pool, 1)

        @block.scalar
        def _(act):
            act.wait_ge(s_memset, 8)

            def row_norms(src, done, c, first=0):
                for j in range(CB):
                    blk = c * CB + j
                    after(act, done, blk - first - 1)
                    nc.scalar.activation(unread[:, blk % 2, 1:D], src[:, blk, 1:D], ACT.Square,
                                         accum_out=sc["ss"][:, blk:blk + 1]).then_inc(done, 1)

            asked = [0]

            def answer(dst, src, func, b, bias=None, own=None, n=KB):
                if own:
                    act.wait_ge(*own)
                else:
                    asked[0] += 1
                    act.wait_ge(s_ask, asked[0])
                nc.scalar.activation(sc[dst][:, b * n:(b + 1) * n], sc[src][:, b * n:(b + 1) * n], func,
                                     **({} if bias is None else {"bias": bias[:, 0:1]})).then_inc(s_answer, 1)

            def norm_sd(c):
                act.wait_ge(s_var, c + 1)
                nc.scalar.activation(sc["sd"][:, c * CB:(c + 1) * CB], sc["var"][:, c * CB:(c + 1) * CB], ACT.Sqrt,
                                     bias=ln_eps[:, 0:1]).then_inc(s_sd, 1)

            def norm_squares(c):
                act.wait_ge(s_clip, c + 1)
                row_norms(y_sb, s_ss, c)

            def log_map(b, stage):
                if stage == 0:
                    answer("y0", "ss", ACT.Sqrt, b, one_eps, own=(s_ss, (b + 1) * KB))
                if stage == 1:
                    answer("u", "t", ACT.Sqrt, b)
                    answer("dn", "inn", ACT.Sqrt, b)
                if stage == 2:
                    answer("d", "w", ACT.Ln, b)

            norm_sd(0)
            for c in range(BC):
                if c + 1 < BC:
                    norm_sd(c + 1)
                norm_squares(c)
            for stage in range(3):
                log_map(0, stage)

            act.wait_ge(s_const, 16 * N_CONST)

            def make_square(c, t):
                act.wait_ge(s_clipped, c * 4 + t + 1)
                after(act, s_norms, c)
                nc.scalar.activation(square[0:SR, t, :], clipped[0:SR, t, :], ACT.Square).then_inc(s_square, 1)

            def part0(c, t):
                after(act, s_store[t], 16 * c)
                nc.scalar.activation(parts[0:SR, t, 0, :], clipped[0:SR, t, :], ACT.Copy).then_inc(s_p0, 1)

            def v_copy(c, n):
                b, cc = c // BC, c % BC
                act.wait_ge(s_vps, c * 2 + n + 1)
                for j in range(2):
                    last = nc.scalar.activation(v_heads[:, b * H:(b + 1) * H, cc * CB + n * 2 + j, :],
                                                ps[:, 6 + n, j * D:(j + 1) * D].rearrange("p (h i) -> p h i", h=H),
                                                ACT.Copy)
                last.then_inc(s_vcopy, 1)

            def make_root(c):
                act.wait_ge(s_norms, c + 1)
                after(act, s_dim0, c - 1)
                nc.scalar.activation(root[:, c % 2, :], ps[0:2 * VW, 2, :], ACT.Sqrt,
                                     bias=one_eps[0:2 * VW, 0:1]).then_inc(s_root, 1)

            def part00(c):
                act.wait_ge(s_dim0, c + 1)
                after(act, s_store0[c % 2], 32 * (c // 2))
                nc.scalar.activation(parts0[:, c % 2, 0, :], dim0[:, c % 2, :], ACT.Copy).then_inc(s_z0, 1)

            def turned(c):
                act.wait_ge(s_tr, c + 1)
                nc.scalar.activation(vT[:, c % 2, :, :], ps[:, 4:6, :], ACT.Copy).then_inc(s_vT, 1)

            turned(0)
            for c in range(CHUNKS):
                make_square(c, 0)
                part0(c, 0)
                if c > 0:
                    make_root(c - 1)
                if c == 2:
                    norm_sd(BC + 3)
                    norm_squares(BC + 1)
                if c == BC - 1:
                    norm_squares(BC + 3)
                    for stage in range(3):
                        log_map(1, stage)
                make_square(c, 1)
                part0(c, 1)
                if c == 0:
                    norm_sd(BC)
                if c == 1:
                    norm_squares(BC)
                v_copy(c, 0)
                if c > 0:
                    part00(c - 1)
                make_square(c, 2)
                part0(c, 2)
                if c == 1:
                    norm_sd(BC + 2)
                v_copy(c, 1)
                make_square(c, 3)
                if c + 1 < CHUNKS:
                    turned(c + 1)
                part0(c, 3)
                if c == 0:
                    norm_sd(BC + 1)
                if c == 2:
                    norm_squares(BC + 2)
            make_root(CHUNKS - 1)

            def exp_map(b):
                answer("u", "ss", ACT.Sqrt, b, eps_col, own=(e_ss, KB) if b == 1 else None)

            def exps(g, first, last=False):
                for kb in range(KB):
                    if last and kb == OUT_ROOT:
                        exp_map(0)
                    if first and kb == 0:
                        act.wait_ge(s_rest, 4 * CHUNKS)
                        act.wait_ge(s_square, 4 * CHUNKS)
                    if first and kb == 1:
                        act.wait_ge(s_p2, 4 * CHUNKS)
                        part00(CHUNKS - 1)
                    if first and kb == 2:
                        act.wait_ge(s_z2, CHUNKS)
                    if first and kb == 3:
                        for n in range(2):
                            act.wait_ge(s_store0[n], 32 * CHUNKS // 2)
                    for half in range(2):
                        act.wait_ge(s_scores, g * (2 * KB) + (kb * 2 + half + 1))
                        if not first or kb >= 4:
                            act.wait_ge(s_pv, g * KB + (kb - 3))
                        nc.scalar.activation(
                            probs[:, kb % 4, half * 2 * CT:(half + 1) * 2 * CT].rearrange("p (a q) -> p a q", a=2),
                            ps[:, half * 2:half * 2 + 2, :], ACT.Exp, scale=DH ** -0.5).then_inc(s_exp, 1)

            exps(0, True)
            with act.Fori(0, HEADS // 2 - 1) as i:
                exps(i * 2 + 1, False)
                exps(i * 2 + 2, False)
            exps(HEADS - 1, False, True)

            def out_vT(c):
                act.wait_ge(e_tr, c + 1)
                after(act, e_wo, 2 * (c - 1))
                nc.scalar.activation(vT[:, c % 2, :, :], ps[:, 4:6, :], ACT.Copy).then_inc(e_trc, 1)

            def out(c):
                if c + 1 < CHUNKS:
                    out_vT(c + 1)
                for n in range(2):
                    act.wait_ge(e_wo, c * 2 + n + 1)
                    nc.scalar.activation(blocks(v_sb, c * CB + n * 2, 2), ps[:, 6 + n, :], ACT.Copy).then_inc(e_woc, 1)
                act.wait_ge(e_woc, c * 2 + 2)
                row_norms(v_sb, e_ss, c, KB)

            def out_norm(b):
                answer("y0", "inn", ACT.Sqrt, b, one_eps)
                answer("sd", "var", ACT.Sqrt, b, ln_eps)

            def token_norm(b, n=KB):
                answer("sd", "var", ACT.Sqrt, b, ln_eps, n=n)

            def to_xT(c):
                par = c % 2
                act.wait_ge(f_tr, c + 1)
                after(act, f_mix, 2 * (c - 1))
                if c:
                    act.wait_ge(f_xT, 2 * c)
                nc.scalar.activation(xT[:, par, :, 0], zero_col[:, :] if c % BC == 0 else xT[:, 1 - par, :, CT],
                                     ACT.Copy).then_inc(f_xT, 1)
                nc.scalar.activation(xT[:, par, :, 1:CT + 1], ps[:, 4:6, :], ACT.Copy).then_inc(f_xT, 1)
                act.wait_ge(f_xT, 2 * c + 2)
                for w in range(2):
                    for k in range(KT):
                        last = nc.scalar.activation(mix_prev[:, par, w, k, :], xT[:, par, k, 0:CT], ACT.Copy,
                                                    scale=omu_sb[:, w, k:k + 1])
                    last.then_inc(f_prev, 1)

            def relu_squares(c):
                after(act, f_sq, c * KT)
                for dt in range(KT):
                    act.wait_ge(f_k, c * KT + dt + 1)
                    nc.scalar.activation(square[:, dt, :], ps[:, 2 + dt, :], ACT.Relu).then_inc(f_relu, 1)
                after(act, f_kv, c * 2)
                for dt in range(KT):
                    act.wait_ge(f_relu, c * KT + dt + 1)
                    nc.scalar.activation(square[:, 2 + dt, :], square[:, dt, :], ACT.Square).then_inc(f_sq, 1)

            def gate(c):
                act.wait_ge(f_r, c + 1)
                after(act, f_o, c - 1)
                nc.scalar.activation(vT[:, c % 2, :, :], ps[:, 0:2, :], ACT.Sigmoid).then_inc(f_sig, 1)

            answer("y0", "inn", ACT.Sqrt, 0, one_eps)
            out_vT(BC)
            answer("sd", "var", ACT.Sqrt, 0, ln_eps)
            out(BC)
            out(BC + 1)
            token_norm(0)
            out(BC + 2)
            act.wait_ge(s_omu, 1)
            to_xT(0)
            out(BC + 3)
            exp_map(1)
            for c in range(CHUNKS):
                if c + 1 < CHUNKS and c not in (2, 3, 4):
                    to_xT(c + 1)
                relu_squares(c)
                if c == 5:
                    token_norm(0)
                gate(c)
                if c == 1:
                    to_xT(3)
                    out_norm(1)
                if c == 2:
                    token_norm(2, 2 * CB)
                if c == 3:
                    to_xT(4)
                    token_norm(3, 2 * CB)
                if c == 4:
                    to_xT(5)
                if c == BC + 2:
                    token_norm(2, 2 * CB)
                if c == BC + 3:
                    token_norm(CHUNKS - 2, CB)
            token_norm(CHUNKS - 1, CB)

        @block.vector
        def _(dve):
            links = [0]

            def link(ins):
                links[0] += 1
                ins.then_inc(s_link, 1)
                dve.wait_ge(s_link, links[0])

            def small(name, b, n=KB):
                return sc[name][:, b * n:(b + 1) * n]

            def layer_stats(src, done, c, first=0):
                for j in range(CB):
                    last = nc.vector.bn_stats(stats[:, c * CB + j, :], src[:, c * CB + j, first:D])
                last.then_inc(done, 1)

            def statistic(n, b, size):
                return stats[:, b * size:(b + 1) * size, n:n + 1].rearrange("p n o -> p (n o)")

            def combine_stats(b, size=KB):
                even, odd, m2_even, m2_odd = (statistic(n, b, size) for n in (1, 4, 2, 5))
                a, w, z, mean = (small(n, b, size) for n in ("a", "w", "z", "mean"))
                nc.vector.tensor_tensor(a, even, odd, ALU.subtract)
                nc.vector.tensor_tensor(w, m2_even, m2_odd, ALU.add)
                link(nc.vector.tensor_tensor(z, even, odd, ALU.add))
                nc.vector.tensor_scalar(mean, z, 0.5, None, ALU.mult)
                link(nc.vector.scalar_tensor_tensor(a, a, 0.25, a, ALU.mult, ALU.mult))
                return nc.vector.scalar_tensor_tensor(small("var", b, size), w, 1.0 / D, a, ALU.mult, ALU.add)

            answers = [0]

            def ask(ins):
                ins.then_inc(s_ask, 1)

            def wait_answer():
                answers[0] += 1
                dve.wait_ge(s_answer, answers[0])

            dve.wait_ge(s_memset, 8)

            def norm_stats(c):
                dve.wait_ge(s_x[c], 16)
                layer_stats(x_sb, s_bn, c)
                dve.wait_ge(s_bn, c + 1)
                combine_stats(c, CB).then_inc(s_var, 1)

            def norm(c, half=None):
                if half != 1:
                    dve.wait_ge(s_sd, c + 1)
                    link(nc.vector.reciprocal(small("rstd", c, CB), small("sd", c, CB)))
                for j in range(0 if half != 1 else CB // 2, CB if half != 0 else CB // 2):
                    blk = c * CB + j
                    last = nc.vector.tensor_scalar(y_sb[:, blk, :], x_sb[:, blk, :], sc["mean"][:, blk:blk + 1],
                                                   sc["rstd"][:, blk:blk + 1], ALU.subtract, ALU.mult)
                if half == 0:
                    return
                last.then_inc(s_norm, 1)
                dve.wait_ge(s_norm, c + 1)
                nc.vector.tensor_scalar(blocks(y_sb, c * CB, CB), blocks(y_sb, c * CB, CB),
                                        8.0, -8.0, ALU.min, ALU.max).then_inc(s_clip, 1)

            def log_map(b, stage):
                s = {n: small(n, b) for n in sc}
                if stage == 1:
                    wait_answer()
                    ask(nc.vector.tensor_tensor(s["w"], s["z"], s["u"], ALU.add))
                    dims0 = y_sb[:, b * KB:(b + 1) * KB, 0:1].rearrange("p n o -> p (n o)")
                    link(nc.vector.tensor_copy(dims0, s["d0"]))
                    wait_answer()
                    link(nc.vector.tensor_scalar(s["dn"], s["dn"], EPS, None, ALU.add))
                    link(nc.vector.reciprocal(s["dn"], s["dn"]))
                if stage == 2:
                    wait_answer()
                    link(nc.vector.scalar_tensor_tensor(s["f"], s["d"], 0.001, s["dn"], ALU.max, ALU.mult))
                if stage > 0:
                    return
                wait_answer()
                link(nc.vector.tensor_scalar(s["z"], s["y0"], 1.0 + EPS, None, ALU.max))
                link(nc.vector.tensor_scalar(s["dn"], s["z"], -1.0, None, ALU.add))
                ask(nc.vector.scalar_tensor_tensor(s["t"], s["z"], 1.0, s["dn"], ALU.add, ALU.mult))
                link(nc.vector.tensor_tensor(s["d0"], s["y0"], s["z"], ALU.subtract))
                link(nc.vector.tensor_tensor(s["a"], s["d0"], s["d0"], ALU.mult))
                link(nc.vector.tensor_tensor(s["inn"], s["ss"], s["a"], ALU.subtract))
                ask(nc.vector.tensor_scalar(s["inn"], s["inn"], EPS, None, ALU.max))

            norm_stats(0)
            for c in range(BC):
                if c + 1 < BC:
                    norm_stats(c + 1)
                norm(c)
            for stage in range(3):
                log_map(0, stage)

            dve.wait_ge(s_const, 16 * N_CONST)
            nc.vector.tensor_scalar(omu_sb[:, :, :], mu_sb[:, :, :], -1.0, 1.0, ALU.mult, ALU.add).then_inc(s_omu, 1)

            def to_token(c):
                after(dve, s_tr, c - 1)
                for j in range(CB):
                    blk = c * CB + j
                    last = nc.vector.tensor_scalar(token[:, c % 2, j, :], y_sb[:, blk, :],
                                                   sc["f"][:, blk:blk + 1], None, ALU.mult)
                last.then_inc(s_token, 1)

            def clip(c, t):
                dve.wait_ge(s_proj, c * 4 + t + 1)
                after(dve, s_rest, (c - 1) * 4 + t + 1)
                after(dve, s_square, (c - 1) * 4 + t + 1)
                nc.vector.tensor_scalar(clipped[0:SR, t, :], ps[0:SR, t % 2, :], -5.0, 5.0,
                                        ALU.max, ALU.min).then_inc(s_clipped, 1)

            def later_parts(c, t):
                dve.wait_ge(s_rest, c * 4 + t + 1)
                nc.vector.tensor_copy(parts[0:SR, t, 1, :], rest[0:SR, t, :]).then_inc(s_p1, 1)
                dve.wait_ge(s_p1, c * 4 + t + 1)
                nc.vector.tensor_tensor(parts[0:SR, t, 2, :], rest[0:SR, t, :], parts[0:SR, t, 1, :],
                                        ALU.subtract).then_inc(s_p2, 1)

            def sign(c):
                dve.wait_ge(s_root, c + 1)
                after(dve, s_z2, c - 1)
                nc.vector.tensor_scalar(dim0[:, c % 2, :], root[:, c % 2, :], sign_sb[:, 0:1], None,
                                        ALU.mult).then_inc(s_dim0, 1)

            def later_parts0(c):
                dve.wait_ge(s_zrest, c + 1)
                nc.vector.tensor_copy(parts0[:, c % 2, 1, :], dim0[:, c % 2, :]).then_inc(s_z1, 1)
                dve.wait_ge(s_z1, c + 1)
                nc.vector.tensor_tensor(parts0[:, c % 2, 2, :], dim0[:, c % 2, :], parts0[:, c % 2, 1, :],
                                        ALU.subtract).then_inc(s_z2, 1)

            def sum_groups(g, m, loaded):
                dve.wait_ge(s_k[m % 3], loaded)
                for n in range(2):
                    last = nc.vector.tensor_tensor(half_sums[:, n, :], kT[m % 3][0:ROWS, 2 * n * NG:(2 * n + 1) * NG],
                                                   kT[m % 3][0:ROWS, (2 * n + 1) * NG:(2 * n + 2) * NG], ALU.add)
                last.then_inc(s_half, 1)
                dve.wait_ge(s_half, g + 1)
                nc.vector.tensor_tensor(group_sums[:, m % 2, :], half_sums[:, 0, :], half_sums[:, 1, :],
                                        ALU.add).then_inc(s_gsum, 1)

            def max_groups(g, m, j, bank):
                dve.wait_ge(s_gps, g * KB + (j + 1))
                nc.vector.tensor_reduce(group_max[:, m % 2, j:j + 1], ps[:, bank, :], AX_X,
                                        ALU.max).then_inc(s_gmax, 1)

            def set_shift(g, m, bank):
                dve.wait_ge(s_shT, g + 1)
                nc.vector.tensor_scalar(shift_row[:, :], ps[0:KB, bank, 0:P], -1.0 / GROUP, -SHIFT * DH ** 0.5,
                                        ALU.mult, ALU.add).then_inc(s_shrow, 1)
                dve.wait_ge(s_shrow, g + 1)
                for half in range(2):
                    js = slice(half * KB // 2, (half + 1) * KB // 2)
                    nc.vector.tensor_tensor(qT[m % 3][ROWS:ROWS + KB, :].rearrange("r (j q) -> r j q", j=KB)[:, js, :],
                                            shift_row[:, :].unsqueeze(1).broadcast_to([KB, KB // 2, P]),
                                            diag_sb[:, js].unsqueeze(2).broadcast_to([KB, KB // 2, P]),
                                            ALU.mult).then_inc(s_shift, 1)

            def norm_step(c, step):
                n = NORM_STEPS.get((c, step))
                if n and n[1] == "stats":
                    norm_stats(n[0])
                elif n:
                    norm(n[0], n[1])

            def first_maxima(c, step):
                for j in GROUPS_AT.get((c, step), ()):
                    max_groups(0, 0, j, 3)

            to_token(0)
            to_token(1)
            for c in range(CHUNKS):
                clip(c, 0)
                first_maxima(c, 0)
                clip(c, 1)
                if c > 0:
                    sign(c - 1)
                if c == BC + 1:
                    sum_groups(0, 0, 16 * LOADS)
                first_maxima(c, 1)
                if c == BC - 1:
                    for stage in range(3):
                        log_map(1, stage)
                    to_token(c + 1)
                    clip(c, 2)
                    clip(c, 3)
                later_parts(c, 0)
                first_maxima(c, 2)
                norm_step(c, 0)
                if c != BC - 1:
                    clip(c, 2)
                first_maxima(c, 3)
                later_parts(c, 1)
                first_maxima(c, 4)
                if c != BC - 1:
                    clip(c, 3)
                norm_step(c, 1)
                if c + 1 < CHUNKS:
                    first_maxima(c, 5)
                else:
                    set_shift(0, 0, 3)
                if c > 0:
                    later_parts0(c - 1)
                later_parts(c, 2)
                norm_step(c, 2)
                later_parts(c, 3)
                norm_step(c, 3)
                if c != BC - 2 and c + 2 < CHUNKS:
                    to_token(c + 2)
            sign(CHUNKS - 1)
            later_parts0(CHUNKS - 1)

            def exp_map(b):
                s = {n: small(n, b) for n in sc}
                if b == 0:
                    even, odd, m2_even, m2_odd = (statistic(n, b, KB) for n in (1, 4, 2, 5))
                    dve.wait_ge(e_bn0, BC)
                    nc.vector.scalar_tensor_tensor(s["a"], even, float(D // 2), even, ALU.mult, ALU.mult)
                    nc.vector.scalar_tensor_tensor(s["t"], odd, float(D // 2 - 1), odd, ALU.mult, ALU.mult)
                    link(nc.vector.tensor_tensor(s["ss"], m2_even, m2_odd, ALU.add))
                    link(nc.vector.tensor_tensor(s["a"], s["a"], s["t"], ALU.add))
                    ask(nc.vector.tensor_tensor(s["ss"], s["ss"], s["a"], ALU.add))
                wait_answer()
                link(nc.vector.tensor_scalar(s["u"], s["u"], 5.0, None, ALU.min))
                nc.vector.tensor_scalar(s["dn"], s["u"], EPS, None, ALU.add)
                link(nc.vector.tensor_tensor(s["t"], s["u"], s["u"], ALU.mult))
                nc.vector.reciprocal(s["dn"], s["dn"])
                link(nc.vector.tensor_scalar(s["a"], s["t"], 1.0 / factorial(2 * SINH_TERMS + 1), None, ALU.mult))
                for k in range(SINH_TERMS - 1, 0, -1):
                    link(nc.vector.scalar_tensor_tensor(s["a"], s["a"], 1.0 / factorial(2 * k + 1), s["t"],
                                                        ALU.add, ALU.mult))
                link(nc.vector.tensor_tensor(s["dn"], s["dn"], s["u"], ALU.mult))
                link(nc.vector.scalar_tensor_tensor(s["f"], s["a"], 1.0, s["dn"], ALU.add, ALU.mult))
                link(nc.vector.reciprocal(s["d"], s["f"]))
                nc.vector.tensor_scalar(s["hi"], s["d"], 8.0, None, ALU.mult)
                link(nc.vector.tensor_scalar(s["lo"], s["d"], -8.0, None, ALU.mult))

            def clip_rows(first, n):
                for c in range(first, first + n):
                    for j in range(CB):
                        blk = c * CB + j
                        last = nc.vector.tensor_scalar(v_sb[:, blk, :], v_sb[:, blk, :], sc["lo"][:, blk:blk + 1],
                                                       sc["hi"][:, blk:blk + 1], ALU.max, ALU.min)
                    last.then_inc(e_clip, 1)
                    dve.wait_ge(e_clip, c + 1)
                    layer_stats(v_sb, e_bn, c, first=1)

            def copy_out(g, m):
                dve.wait_ge(s_pv, g * KB + KB)
                nc.vector.tensor_copy(oT[:, m % 2, :], ps[:, 6 + m % 2, :]).then_inc(s_oT, 1)

            def divide(g, m):
                dve.wait_ge(s_otr, g + 1)
                tokens = ps[:, 6 + m % 2, :].rearrange("p (j c i) -> p j c i", j=CB, c=QC)
                nc.vector.reciprocal(rden[:, m % 2, :, :], tokens[:, :, :, DH:DH + 1].rearrange("p j c o -> p j (c o)")
                                     ).then_inc(s_rden, 1)
                dve.wait_ge(s_rden, g + 1)
                nc.vector.tensor_tensor(
                    o_heads[:, bass.ds(g, 1), :, :].rearrange("p g k i -> p (g k) i").rearrange(
                        "p (c j) i -> p j c i", j=CB),
                    tokens[:, :, :, 0:DH], rden[:, m % 2, :, :].unsqueeze(3).broadcast_to([P, CB, QC, DH]),
                    ALU.mult).then_inc(s_out, 1)

            def head(g, m, first, loaded):
                sum_groups(g + 1, m + 1, loaded)
                if not first:
                    copy_out(g - 1, m - 1)
                for j in range(KB):
                    if j == 1 and not first:
                        divide(g - 1, m - 1)
                    max_groups(g + 1, m + 1, j, 4 + j % 2)
                set_shift(g + 1, m + 1, 4)

            head(0, 0, True, 16 * LOADS)
            with dve.Fori(0, (HEADS - 2) // 6) as i:
                for n in range(1, 7):
                    head(i * 6 + n, n, False, i * (2 * 16 * LOADS) + loads_of(n + 1))

            def turned(c):
                dve.wait_ge(e_tr, c + 1)
                after(dve, e_wo, 2 * (c - 1))
                nc.vector.tensor_copy(vT[:, c % 2, :, :], ps[:, 4:6, :]).then_inc(e_trc, 1)

            copy_out(HEADS - 2, 0)
            turned(0)
            divide(HEADS - 2, 0)
            for c in range(BC):
                if c > 0:
                    turned(c)
                dve.wait_ge(e_wo, c * 2 + 2)
                nc.vector.tensor_copy(blocks(v_sb, c * CB, CB), ps[:, 4:6, :].rearrange("p a b -> p (a b)")
                                      ).then_inc(e_woc, 2)
                dve.wait_ge(e_woc, c * 2 + 2)
                layer_stats(v_sb, e_bn0, c, first=1)
            exp_map(0)
            clip_rows(0, BC)
            copy_out(HEADS - 1, 1)
            divide(HEADS - 1, 1)

            def out_norm(b):
                s = {n: small(n, b) for n in sc}
                even, odd, m2_even, m2_odd = (statistic(n, b, KB) for n in (1, 4, 2, 5))
                ne, no = D // 2, D // 2 - 1
                dve.wait_ge(e_bn, (b + 1) * BC)
                nc.vector.tensor_scalar(s["z"], even, float(ne) / (D - 1), None, ALU.mult)
                nc.vector.tensor_tensor(s["m2"], m2_even, m2_odd, ALU.add)
                link(nc.vector.tensor_tensor(s["a"], even, odd, ALU.subtract))
                nc.vector.scalar_tensor_tensor(s["z"], odd, float(no) / (D - 1), s["z"], ALU.mult, ALU.add)
                link(nc.vector.scalar_tensor_tensor(s["a"], s["a"], float(ne * no) / (D - 1), s["a"],
                                                    ALU.mult, ALU.mult))
                nc.vector.tensor_tensor(s["z"], s["z"], s["f"], ALU.mult)
                nc.vector.tensor_tensor(s["t"], s["f"], s["f"], ALU.mult)
                link(nc.vector.tensor_tensor(s["m2"], s["m2"], s["a"], ALU.add))
                link(nc.vector.tensor_tensor(s["m2"], s["m2"], s["t"], ALU.mult))
                link(nc.vector.scalar_tensor_tensor(s["a"], s["z"], float(D - 1), s["z"], ALU.mult, ALU.mult))
                ask(nc.vector.tensor_tensor(s["inn"], s["m2"], s["a"], ALU.add))
                wait_answer()
                nc.vector.tensor_tensor(s["w"], s["y0"], s["z"], ALU.subtract)
                link(nc.vector.tensor_tensor(v_sb[:, b * KB:(b + 1) * KB, 0:1].rearrange("p n o -> p (n o)"),
                                             s["y0"], s["d"], ALU.mult))
                link(nc.vector.scalar_tensor_tensor(s["a"], s["w"], float(D - 1) / D, s["w"], ALU.mult, ALU.mult))
                link(nc.vector.tensor_tensor(s["var"], s["m2"], s["a"], ALU.add))
                ask(nc.vector.tensor_scalar(s["var"], s["var"], 1.0 / D, None, ALU.mult))
                link(nc.vector.scalar_tensor_tensor(s["mean"], s["w"], 1.0 / D, s["z"], ALU.mult, ALU.add))
                link(nc.vector.tensor_tensor(s["shift"], s["mean"], s["d"], ALU.mult))
                wait_answer()
                link(nc.vector.reciprocal(s["rstd"], s["sd"]))
                link(nc.vector.tensor_tensor(s["scale"], s["rstd"], s["f"], ALU.mult))

            def normalise(dst, src, c, shift="mean", scale="rstd"):
                for j in range(CB):
                    blk = c * CB + j
                    last = nc.vector.tensor_scalar(dst(j), src[:, blk, :], sc[shift][:, blk:blk + 1],
                                                   sc[scale][:, blk:blk + 1], ALU.subtract, ALU.mult)
                return last

            def attention_norm(c):
                normalise(lambda j: v_sb[:, c * CB + j, :], v_sb, c, "shift", "scale").then_inc(e_norm, 1)

            def add_x(c):
                dve.wait_ge(e_norm, c + 1)
                link(nc.vector.tensor_tensor(blocks(x_sb, c * CB, CB), blocks(x_sb, c * CB, CB),
                                             blocks(v_sb, c * CB, CB), ALU.add))

            def x1_stats(c):
                b, cc = c // BC, c % BC
                if cc < X1_POOL:
                    dve.wait_ge(e_x1, b * X1_POOL + cc + 1)
                layer_stats(x_sb, e_bn1, c)

            def ask_sd(b, done, count, n=KB):
                dve.wait_ge(done, count)
                ask(combine_stats(b, n))

            def take_rstd(b, n=KB):
                wait_answer()
                link(nc.vector.reciprocal(small("rstd", b, n), small("sd", b, n)))

            def to_tokens(c):
                after(dve, f_tr, c - 1)
                normalise(lambda j: token[:, c % 2, j, :], x_sb, c).then_inc(f_token, 1)

            def mix(c):
                after(dve, f_r, c - 1)
                for w in (1, 0):
                    dve.wait_ge(f_prev, c * 2 + 2)
                    for k in range(KT):
                        last = nc.vector.scalar_tensor_tensor(mixed[:, c % 2, w, k, :], xT[:, c % 2, k, 1:CT + 1],
                                                              mu_sb[:, w, k:k + 1], mix_prev[:, c % 2, w, k, :],
                                                              ALU.mult, ALU.add)
                    last.then_inc(f_mix, 1)

            def gated(c):
                dve.wait_ge(f_kv, c * 2 + 2)
                dve.wait_ge(f_sig, c + 1)
                nc.vector.tensor_tensor(blocks(y_sb, c * CB, CB), vT[:, c % 2, :, :].rearrange("p a b -> p (a b)"),
                                        ps[:, 6:8, :].rearrange("p a b -> p (a b)"), ALU.mult).then_inc(f_o, 1)
                dve.wait_ge(f_o, c + 1)
                layer_stats(y_sb, f_bn, c)

            def finish(c):
                normalise(lambda j: y_sb[:, c * CB + j, :], y_sb, c).then_inc(f_norm, 1)
                if c < OUT_POOL:
                    return
                dve.wait_ge(f_norm, c + 1)
                nc.vector.tensor_tensor(blocks(y_sb, c * CB, CB), blocks(y_sb, c * CB, CB),
                                        blocks(x_sb, c * CB, CB), ALU.add).then_inc(f_out, 1)

            out_norm(0)
            for c in range(BC):
                attention_norm(c)
            for c in (2, 3):
                add_x(c)
                x1_stats(c)
            x1_stats(0)
            x1_stats(1)
            ask_sd(0, e_bn1, BC)
            take_rstd(0)
            to_tokens(0)
            dve.wait_ge(e_tr, CHUNKS)
            to_tokens(1)
            mix(0)
            exp_map(1)
            to_tokens(2)
            mix(1)
            clip_rows(4, 2)
            mix(2)
            gated(0)
            to_tokens(3)
            clip_rows(6, 2)
            out_norm(1)
            attention_norm(4)
            attention_norm(5)
            mix(3)
            attention_norm(6)
            attention_norm(7)
            gated(1)
            x1_stats(4)
            x1_stats(5)
            ask_sd(2, e_bn1, 6, 2 * CB)
            add_x(6)
            x1_stats(6)
            take_rstd(2, 2 * CB)
            to_tokens(4)
            gated(2)
            add_x(7)
            mix(4)
            x1_stats(7)
            ask_sd(3, e_bn1, 8, 2 * CB)
            take_rstd(3, 2 * CB)
            to_tokens(5)
            gated(3)
            to_tokens(6)
            mix(5)
            to_tokens(7)
            gated(4)
            mix(6)
            ask_sd(0, f_bn, BC)
            take_rstd(0)
            for c in (0, 1, 2):
                finish(c)
            mix(7)
            gated(5)
            ask_sd(2, f_bn, 6, 2 * CB)
            finish(3)
            gated(6)
            take_rstd(2, 2 * CB)
            ask_sd(6, f_bn, 7, CB)
            finish(4)
            finish(5)
            gated(7)
            ask_sd(CHUNKS - 1, f_bn, CHUNKS, CB)
            take_rstd(CHUNKS - 2, CB)
            finish(CHUNKS - 2)
            take_rstd(CHUNKS - 1, CB)
            finish(CHUNKS - 1)

        @block.tensor
        def _(pe):
            pe.wait_ge(s_const, 16 * N_CONST)

            def transposes(par, done):
                for k in range(KT):
                    for j in range(CB):
                        last = nc.tensor.transpose(ps[:, 4 + k, j * P:(j + 1) * P],
                                                   token[:, par, j, k * P:(k + 1) * P], ident_sb[:, :])
                last.then_inc(done, 1)

            def by_token(bank, j, left, w):
                for k in range(KT):
                    last = nc.tensor.matmul(ps[:, bank, (j % 2) * D:(j % 2 + 1) * D], left[:, k, j * P:(j + 1) * P],
                                            w[:, k, :], start=(k == 0), stop=(k == KT - 1))
                return last

            def by_dim(bank, dt, w, right, rows=P):
                for k in range(KT):
                    last = nc.tensor.matmul(ps[0:rows, bank, :], w[:, k, dt * rows:(dt + 1) * rows], right[:, k, :],
                                            start=(k == 0), stop=(k == KT - 1))
                return last

            def turn(c):
                pe.wait_ge(s_token, c + 1)
                after(pe, s_vT, c)
                transposes(c % 2, s_tr)

            def project(c, t):
                after(pe, s_clipped, c * 4 + t - 1)
                by_dim(t % 2, t % 2, w_sb["q" if t < 2 else "k"], vT[:, c % 2], SR).then_inc(s_proj, 1)

            def norms(c):
                pe.wait_ge(s_square, c * 4 + 4)
                after(pe, s_root, c)
                for dt in range(2):
                    for n in range(2):
                        last = nc.tensor.matmul(ps[n * VW:(n + 1) * VW, 2, :], headsum_sb[:, dt, :],
                                                square[0:SR, 2 * n + dt, :], start=(dt == 0), stop=(dt == 1))
                last.then_inc(s_norms, 1)

            def values(c, n):
                after(pe, s_vcopy, (c - 1) * 2 + n + 1)
                for j in range(2):
                    last = by_token(6 + n, 2 * n + j, vT[:, c % 2], w_sb["v"])
                last.then_inc(s_vps, 1)

            def group_scores(g, m, j, bank):
                if j == 0:
                    pe.wait_ge(s_gsum, g + 1)
                    after(pe, s_shrow, g)
                after(pe, s_gmax, g * KB + (j if bank == 3 else j - 1))
                nc.tensor.matmul(ps[:, bank, :], qT[m % 3][0:ROWS, j * P:(j + 1) * P], group_sums[:, m % 2, :],
                                 start=True, stop=True).then_inc(s_gps, 1)

            def turn_max(g, m, bank):
                pe.wait_ge(s_gmax, g * KB + KB)
                nc.tensor.transpose(ps[0:KB, bank, 0:P], group_max[:, m % 2, :], ident_sb[:, :]).then_inc(s_shT, 1)

            def first_groups(c, step):
                for j in GROUPS_AT.get((c, step), ()):
                    group_scores(0, 0, j, 3)

            turn(0)
            for c in range(CHUNKS):
                if c > 0:
                    norms(c - 1)
                pe.wait_ge(s_vT, c + 1)
                project(c, 0)
                first_groups(c, 0)
                project(c, 1)
                first_groups(c, 1)
                values(c, 0)
                if c == BC + 1:
                    pe.wait_ge(s_q[0], 16 * LOADS)
                first_groups(c, 2)
                project(c, 2)
                first_groups(c, 3)
                if c + 1 < CHUNKS:
                    values(c, 1)
                    first_groups(c, 4)
                    project(c, 3)
                    first_groups(c, 5)
                    turn(c + 1)
                else:
                    project(c, 3)
                    turn_max(0, 0, 3)
                    values(c, 1)
            norms(CHUNKS - 1)

            def scores(g, m, kb, half):
                if kb == 0:
                    pe.wait_ge(s_shift, g * 2 + (half + 1))
                after(pe, s_exp, g * (2 * KB) + (kb * 2 + half - 1))
                for n in range(2):
                    q0 = (half * 2 + n) * CT
                    last = nc.tensor.matmul(ps[:, half * 2 + n, :], kT[m % 3][0:ROWS + KB, kb * P:(kb + 1) * P],
                                            qT[m % 3][0:ROWS + KB, q0:q0 + CT], start=True, stop=True)
                last.then_inc(s_scores, 1)

            def weigh(g, m, kb):
                pe.wait_ge(s_exp, g * (2 * KB) + (kb * 2 + 2))
                if kb == 0:
                    pe.wait_ge(s_vhead, g + 1)
                for c in range(QC):
                    last = nc.tensor.matmul(ps[c * VW:(c + 1) * VW, 6 + m % 2, :], v_head[:, m % 2, kb, :],
                                            probs[:, kb % 4, c * CT:(c + 1) * CT], start=(kb == 0), stop=(kb == KB - 1))
                last.then_inc(s_pv, 1)

            def turn_out(g, m):
                pe.wait_ge(s_oT, g + 1)
                for j in range(CB):
                    last = nc.tensor.transpose(ps[:, 6 + m % 2, j * P:(j + 1) * P],
                                               oT[:, m % 2, j * P:(j + 1) * P], ident_sb[:, :])
                last.then_inc(s_otr, 1)

            def turn_attention(c):
                pe.wait_ge(e_token, c + 1)
                after(pe, e_trc, c)
                after(pe, e_woc, 2 * min(c, BC))
                transposes(c % 2, e_tr)

            def out_product(c, bank):
                pe.wait_ge(e_trc, c + 1)
                for n in range(2):
                    after(pe, e_woc, (c - 1) * 2 + n + 1)
                    for j in range(2):
                        last = by_token(bank + n, 2 * n + j, vT[:, c % 2], w_sb["o"])
                    last.then_inc(e_wo, 1)

            def head(g, m, first, last, loaded):
                for kb in range(KB):
                    scores(g, m, kb, 1)
                    if kb > 0:
                        weigh(g, m, kb - 1)
                    elif not first:
                        weigh(g - 1, m - 1, KB - 1)
                    if kb + 1 < KB:
                        scores(g, m, kb + 1, 0)
                    elif not last:
                        scores(g + 1, m + 1, 0, 0)
                    if kb == 1 and not first:
                        turn_out(g - 1, m - 1)
                    if kb == G_FIRST and not last:
                        pe.wait_ge(s_q[(m + 1) % 3], loaded)
                    if G_FIRST <= kb < G_FIRST + G_STEPS and not last:
                        for j in range((kb - G_FIRST) * KB // G_STEPS, (kb - G_FIRST + 1) * KB // G_STEPS):
                            group_scores(g + 1, m + 1, j, 4 + j % 2)
                    if kb == G_FIRST + G_STEPS and not last:
                        turn_max(g + 1, m + 1, 4)
                    if last and kb < 2 * BC:
                        if kb % 2 == 0:
                            turn_attention(kb // 2)
                        else:
                            out_product(kb // 2, 4)

            pe.wait_ge(s_memset, 8)
            pe.wait_ge(s_clipped, 4 * CHUNKS)
            pe.wait_ge(s_root, CHUNKS)
            pe.wait_ge(s_vcopy, 2 * CHUNKS)
            scores(0, 0, 0, 0)
            head(0, 0, True, False, 16 * LOADS)
            pe.wait_ge(s_memset, 9)
            with pe.Fori(0, (HEADS - 2) // 6) as i:
                for n in range(1, 7):
                    head(i * 6 + n, n, False, False, i * (2 * 16 * LOADS) + loads_of(n + 1))
            head(HEADS - 1, 1, False, True, 0)
            weigh(HEADS - 1, 1, KB - 1)
            turn_out(HEADS - 1, 1)

            def turn_tokens(c):
                pe.wait_ge(f_token, c + 1)
                after(pe, f_xT, 2 * c)
                transposes(c % 2, f_tr)

            pe.wait_ge(s_out, HEADS)
            turn_attention(BC)
            for c in range(BC, CHUNKS):
                pe.wait_ge(e_trc, c + 1)
                if c + 1 < CHUNKS:
                    turn_attention(c + 1)
                else:
                    turn_tokens(0)
                out_product(c, 6)

            turn_tokens(1)
            pe.wait_ge(e_woc, 2 * CHUNKS)

            def product_k(c):
                pe.wait_ge(f_mix, 2 * c + 1)
                for dt in range(KT):
                    after(pe, f_relu, (c - 1) * KT + dt + 1)
                    by_dim(2 + dt, dt, w_sb["kf"], mixed[:, c % 2, 1]).then_inc(f_k, 1)

            def product_r(c):
                pe.wait_ge(f_mix, 2 * c + 2)
                after(pe, f_sig, c)
                for j in range(CB):
                    last = by_token(j // 2, j, mixed[:, c % 2, 0], w_sb["r"])
                last.then_inc(f_r, 1)

            def product_kv(c):
                pe.wait_ge(f_sq, c * KT + KT)
                after(pe, f_o, c)
                for n in range(2):
                    for j in range(2):
                        last = by_token(6 + n, 2 * n + j, square[:, 2:4], w_sb["vf"])
                    last.then_inc(f_kv, 1)

            product_k(0)
            product_r(0)
            for c in range(CHUNKS):
                late = c in (2, 3)
                if c + 2 < CHUNKS and not late and c != 4:
                    turn_tokens(c + 2)
                if c in (3, 4):
                    product_kv(c)
                if c == 4:
                    turn_tokens(c + 2)
                if c + 1 < CHUNKS:
                    product_k(c + 1)
                if c not in (3, 4):
                    product_kv(c)
                if c + 1 < CHUNKS:
                    product_r(c + 1)
                if late:
                    turn_tokens(c + 2)


def kernel(L0_attn_x, L0_attn_Wq, L0_attn_Wk, L0_attn_Wv, L0_attn_Wo, L0_ffn_W_r, L0_ffn_W_k, L0_ffn_W_v,
           L0_ffn_mu_r, L0_ffn_mu_k):
    import numpy as np
    import concourse.bacc as bacc
    from concourse.bass_utils import run_bass_kernel_spmd

    ident = np.eye(P, dtype=np.float32)
    row = np.arange(2 * SR).reshape(2, SR).T
    headsum = (row[:, :, None] % H == np.arange(VW)).astype(np.float32)
    sign = np.where(np.arange(2 * VW) < VW, -1.0, 1.0).astype(np.float32)[:, None]

    def dim_major(w):
        return np.ascontiguousarray(np.asarray(w).reshape(H, DH, D)[:, 1:].transpose(2, 1, 0).reshape(D, 2 * SR))

    arrays = {
        "x": np.ascontiguousarray(L0_attn_x).reshape(B * T, D),
        "wq": dim_major(L0_attn_Wq),
        "wk": dim_major(L0_attn_Wk),
        "wv": np.ascontiguousarray(np.asarray(L0_attn_Wv).T),
        "wo": np.ascontiguousarray(np.asarray(L0_attn_Wo).T),
        "wr": np.ascontiguousarray(np.asarray(L0_ffn_W_r).T),
        "wkf": np.ascontiguousarray(np.asarray(L0_ffn_W_k).T),
        "wvf": np.ascontiguousarray(np.asarray(L0_ffn_W_v).T),
        "mus": np.ascontiguousarray(np.stack([np.asarray(m).reshape(KT, P).T for m in (L0_ffn_mu_r, L0_ffn_mu_k)], 1)),
        "ident": ident, "headsum": headsum, "sign": sign, "diag": np.eye(KB, dtype=np.float32),
    }
    nc = bacc.Bacc("TRN2", target_bir_lowering=False, num_devices=1)
    args = [nc.dram_tensor(f"in_{n}", a.shape, mybir.dt.from_np(a.dtype), kind="ExternalInput").ap()
            for n, a in arrays.items()]
    args.append(nc.dram_tensor("out_0", (B * T, D), F32, kind="ExternalOutput").ap())
    sandwich(nc, *args)
    r = run_bass_kernel_spmd(nc, [{f"in_{n}": a for n, a in arrays.items()}], core_ids=[0])
    return r.results[0]["out_0"].reshape(B, T, D)
```
